# Optimizing a Trainium2 kernel written in Bass

```python
import numpy as np
import jax
import jax.numpy as jnp

def _softmax(x, axis=-1):
    return jax.nn.softmax(x, axis=axis)
def _gelu(x):
    return jax.nn.gelu(x, approximate=True)
def _silu(x):
    return jax.nn.silu(x)
def _sigmoid(x):
    return jax.nn.sigmoid(x)
def _layernorm(x, axis=-1, eps=1e-5):
    m = jnp.mean(x, axis=axis, keepdims=True)
    v = jnp.var(x, axis=axis, keepdims=True)
    return (x - m) / jnp.sqrt(v + eps)
def _scatter_add(tgt, idx, src, axis=0):
    return tgt.at[idx].add(src)
def _segment_sum(src, seg, n):
    return jax.ops.segment_sum(src, seg, n)

kernel_name = 'mk_conv_seq_d2_conv_nchw128_babe28'

def setup_inputs(seed: int = 0):
    np.random.seed(seed)
    _w = jnp.asarray
    def _rec_inputs():
        import jax
        import jax.numpy as jnp
        _gk = jax.random.key(seed)
        x = -0.0003929 + 0.9999 * jax.random.normal(jax.random.fold_in(_gk, 1), (8, 128, 128, 128), jnp.float32)
        return x
    x = _rec_inputs()
    def _L0_conv_setup():
        import jax, jax.numpy as jnp
        import numpy as np
        B, C, H, W = (8, 128, 128, 128)
        GS = 8
        HID = 256

        def _conv1x1(t, Wm, bm):
            return jnp.einsum('bchw,oc->bohw', t, Wm) + bm[None, :, None, None]
        key = jax.random.key(seed)
        ks = jax.random.split(key, 7)
        s = 1.0 / np.sqrt(C)
        sh = 1.0 / np.sqrt(HID)
        return {'x': jax.random.normal(ks[0], (B, C, H, W), jnp.float32), 'Wq': jax.random.normal(ks[1], (C, C), jnp.float32) * s, 'bq': jnp.zeros((C,), jnp.float32), 'Wk': jax.random.normal(ks[2], (C, C), jnp.float32) * s, 'bk': jnp.zeros((C,), jnp.float32), 'Wv': jax.random.normal(ks[3], (C, C), jnp.float32) * s, 'bv': jnp.zeros((C,), jnp.float32), 'W1': jax.random.normal(ks[4], (HID, C), jnp.float32) * s, 'b1': jnp.zeros((HID,), jnp.float32), 'W2': jax.random.normal(ks[5], (C, HID), jnp.float32) * sh, 'b2': jnp.zeros((C,), jnp.float32)}
    _L0_conv_all = _L0_conv_setup()
    _L0_conv_in = {k: v for k, v in _L0_conv_all.items() if k in ('Wq', 'bq', 'Wk', 'bk', 'Wv', 'bv', 'W1', 'b1', 'W2', 'b2', )}
    del _L0_conv_all

    def _L1_conv_setup():
        import jax, jax.numpy as jnp
        import numpy as np
        from jax import lax
        B, DIM, H, W = (2, 128, 128, 128)
        GC, NSET, K = (2, 16, 3)
        G = DIM // GC
        KK = K * K
        INTERC = min(DIM, 16)

        def _conv(x, w, b, pad, groups=1):
            y = lax.conv_general_dilated(x, w, (1, 1), [(pad, pad), (pad, pad)], dimension_numbers=('NCHW', 'OIHW', 'NCHW'), feature_group_count=groups)
            return y + b[None, :, None, None]

        def _kba(xin, att, selfb, selfw):
            Bb, C, Hh, Ww = xin.shape
            P = Hh * Ww
            att2 = att.reshape(Bb, NSET, P).transpose(0, 2, 1)
            bias = jnp.einsum('bpn,nc->bpc', att2, selfb[0])
            attk = jnp.einsum('bpn,nm->bpm', att2, selfw[0])
            attk = attk.reshape(Bb, P, G, GC, GC * KK)
            pad = K // 2
            xp = jnp.pad(xin, ((0, 0), (0, 0), (pad, pad), (pad, pad)))
            patches = jnp.stack([xp[:, :, i:i + Hh, j:j + Ww] for i in range(K) for j in range(K)], axis=2)
            uf = patches.reshape(Bb, G, GC * KK, P).transpose(0, 3, 1, 2)
            y = jnp.einsum('bpgij,bpgj->bpgi', attk, uf).reshape(Bb, P, C) + bias
            return y.transpose(0, 2, 1).reshape(Bb, C, Hh, Ww)
        key = jax.random.key(seed)
        ks = jax.random.split(key, 13)
        f = lambda k, s: jax.random.normal(k, s, jnp.float32) * 0.05
        return {'x': jax.random.normal(ks[0], (B, DIM, H, W), jnp.float32), 'w_conv1_pw': f(ks[1], (DIM, DIM, 1, 1)), 'b_conv1_pw': f(ks[2], (DIM,)), 'w_conv1_dw': f(ks[3], (DIM, 1, 3, 3)), 'b_conv1_dw': f(ks[4], (DIM,)), 'w_conv2_g': f(ks[5], (INTERC, DIM // INTERC, 3, 3)), 'b_conv2_g': f(ks[6], (INTERC,)), 'w_conv2_pw': f(ks[7], (NSET, INTERC // 2, 1, 1)), 'b_conv2_pw': f(ks[8], (NSET,)), 'w_conv211': f(ks[9], (NSET, DIM, 1, 1)), 'b_conv211': f(ks[10], (NSET,)), 'attgamma': jnp.full((1, NSET, 1, 1), 0.01, jnp.float32), 'ga1': jnp.full((1, DIM, 1, 1), 0.01, jnp.float32), 'selfb': f(ks[11], (1, NSET, DIM)), 'selfw': f(ks[12], (1, NSET, DIM * GC * KK))}
    _L1_conv_all = _L1_conv_setup()
    _L1_conv_in = {k: v for k, v in _L1_conv_all.items() if k in ('w_conv1_pw', 'b_conv1_pw', 'w_conv1_dw', 'b_conv1_dw', 'w_conv2_g', 'b_conv2_g', 'w_conv2_pw', 'b_conv2_pw', 'w_conv211', 'b_conv211', 'attgamma', 'ga1', 'selfb', 'selfw', )}
    del _L1_conv_all

    return {
        "x": x,
        "L0_conv_Wq": _L0_conv_in["Wq"],
        "L0_conv_bq": _L0_conv_in["bq"],
        "L0_conv_Wk": _L0_conv_in["Wk"],
        "L0_conv_bk": _L0_conv_in["bk"],
        "L0_conv_Wv": _L0_conv_in["Wv"],
        "L0_conv_bv": _L0_conv_in["bv"],
        "L0_conv_W1": _L0_conv_in["W1"],
        "L0_conv_b1": _L0_conv_in["b1"],
        "L0_conv_W2": _L0_conv_in["W2"],
        "L0_conv_b2": _L0_conv_in["b2"],
        "L1_conv_w_conv1_pw": _L1_conv_in["w_conv1_pw"],
        "L1_conv_b_conv1_pw": _L1_conv_in["b_conv1_pw"],
        "L1_conv_w_conv1_dw": _L1_conv_in["w_conv1_dw"],
        "L1_conv_b_conv1_dw": _L1_conv_in["b_conv1_dw"],
        "L1_conv_w_conv2_g": _L1_conv_in["w_conv2_g"],
        "L1_conv_b_conv2_g": _L1_conv_in["b_conv2_g"],
        "L1_conv_w_conv2_pw": _L1_conv_in["w_conv2_pw"],
        "L1_conv_b_conv2_pw": _L1_conv_in["b_conv2_pw"],
        "L1_conv_w_conv211": _L1_conv_in["w_conv211"],
        "L1_conv_b_conv211": _L1_conv_in["b_conv211"],
        "L1_conv_attgamma": _L1_conv_in["attgamma"],
        "L1_conv_ga1": _L1_conv_in["ga1"],
        "L1_conv_selfb": _L1_conv_in["selfb"],
        "L1_conv_selfw": _L1_conv_in["selfw"],
    }

def reference(x, L0_conv_Wq, L0_conv_bq, L0_conv_Wk, L0_conv_bk, L0_conv_Wv, L0_conv_bv, L0_conv_W1, L0_conv_b1, L0_conv_W2, L0_conv_b2, L1_conv_w_conv1_pw, L1_conv_b_conv1_pw, L1_conv_w_conv1_dw, L1_conv_b_conv1_dw, L1_conv_w_conv2_g, L1_conv_b_conv2_g, L1_conv_w_conv2_pw, L1_conv_b_conv2_pw, L1_conv_w_conv211, L1_conv_b_conv211, L1_conv_attgamma, L1_conv_ga1, L1_conv_selfb, L1_conv_selfw):
    import jax
    import jax.numpy as jnp
    def _L0_conv_ref(x, Wq, bq, Wk, bk, Wv, bv, W1, b1, W2, b2):
        import jax, jax.numpy as jnp
        import numpy as np
        B, C, H, W = (8, 128, 128, 128)
        GS = 8
        HID = 256

        def _conv1x1(t, Wm, bm):
            return jnp.einsum('bchw,oc->bohw', t, Wm) + bm[None, :, None, None]
        Bs, Cs, Hs, Ws = x.shape
        gh, gw = (Hs // GS, Ws // GS)
        G = gh * gw

        def to_grid(t):
            t = t.reshape(Bs, Cs, gh, GS, gw, GS)
            t = t.transpose(0, 2, 4, 1, 3, 5)
            return t.reshape(Bs, G, Cs, GS * GS)
        q = to_grid(_conv1x1(x, Wq, bq))
        k = to_grid(_conv1x1(x, Wk, bk))
        v = to_grid(_conv1x1(x, Wv, bv))
        attn = jnp.einsum('bgck,bgcl->bgkl', q, k) / np.sqrt(Cs).astype(np.float32)
        attn = jax.nn.softmax(attn, axis=-1)
        out = jnp.einsum('bgkl,bgcl->bgck', attn, v)
        out = out.reshape(Bs, gh, gw, Cs, GS, GS)
        out = out.transpose(0, 3, 1, 4, 2, 5).reshape(Bs, Cs, Hs, Ws)
        x = x + out
        h = jax.nn.gelu(_conv1x1(x, W1, b1), approximate=False)
        x = x + _conv1x1(h, W2, b2)
        return x

    def _L1_conv_ref(x, w_conv1_pw, b_conv1_pw, w_conv1_dw, b_conv1_dw, w_conv2_g, b_conv2_g, w_conv2_pw, b_conv2_pw, w_conv211, b_conv211, attgamma, ga1, selfb, selfw):
        import jax, jax.numpy as jnp
        import numpy as np
        from jax import lax
        B, DIM, H, W = (2, 128, 128, 128)
        GC, NSET, K = (2, 16, 3)
        G = DIM // GC
        KK = K * K
        INTERC = min(DIM, 16)

        def _conv(x, w, b, pad, groups=1):
            y = lax.conv_general_dilated(x, w, (1, 1), [(pad, pad), (pad, pad)], dimension_numbers=('NCHW', 'OIHW', 'NCHW'), feature_group_count=groups)
            return y + b[None, :, None, None]

        def _kba(xin, att, selfb, selfw):
            Bb, C, Hh, Ww = xin.shape
            P = Hh * Ww
            att2 = att.reshape(Bb, NSET, P).transpose(0, 2, 1)
            bias = jnp.einsum('bpn,nc->bpc', att2, selfb[0])
            attk = jnp.einsum('bpn,nm->bpm', att2, selfw[0])
            attk = attk.reshape(Bb, P, G, GC, GC * KK)
            pad = K // 2
            xp = jnp.pad(xin, ((0, 0), (0, 0), (pad, pad), (pad, pad)))
            patches = jnp.stack([xp[:, :, i:i + Hh, j:j + Ww] for i in range(K) for j in range(K)], axis=2)
            uf = patches.reshape(Bb, G, GC * KK, P).transpose(0, 3, 1, 2)
            y = jnp.einsum('bpgij,bpgj->bpgi', attk, uf).reshape(Bb, P, C) + bias
            return y.transpose(0, 2, 1).reshape(Bb, C, Hh, Ww)
        enh = _conv(_conv(x, w_conv1_pw, b_conv1_pw, 0), w_conv1_dw, b_conv1_dw, 1, groups=DIM)
        h = _conv(x, w_conv2_g, b_conv2_g, 1, groups=INTERC)
        h1, h2 = jnp.split(h, 2, axis=1)
        attn = _conv(h1 * h2, w_conv2_pw, b_conv2_pw, 0) * attgamma + _conv(x, w_conv211, b_conv211, 0)
        x2 = _kba(enh, attn, selfb, selfw) * ga1 + enh
        return x2 + x

    def _gn(v, G=32, eps=1e-5):
        B_, C_, H_, W_ = v.shape
        g = v.reshape(B_, G, C_ // G, H_, W_)
        m = jnp.mean(g, axis=(2, 3, 4), keepdims=True)
        s = jnp.var(g, axis=(2, 3, 4), keepdims=True)
        return ((g - m) / jnp.sqrt(s + eps)).reshape(v.shape)

    def _ln_c(v, eps=1e-6):
        m = jnp.mean(v, axis=1, keepdims=True)
        s = jnp.var(v, axis=1, keepdims=True)
        return (v - m) / jnp.sqrt(s + eps)

    def _ln_t(v, eps=1e-5):
        m = jnp.mean(v, axis=-1, keepdims=True)
        s = jnp.var(v, axis=-1, keepdims=True)
        return (v - m) / jnp.sqrt(s + eps)

    def _to_tokens(v):
        B_, C_, H_, W_ = v.shape
        return v.reshape(B_, C_, H_ * W_).transpose(0, 2, 1)
    def _from_tokens(t, like):
        B_, C_, H_, W_ = like.shape
        return t.transpose(0, 2, 1).reshape(B_, C_, H_, W_)

    x = _L0_conv_ref(x, L0_conv_Wq, L0_conv_bq, L0_conv_Wk, L0_conv_bk, L0_conv_Wv, L0_conv_bv, L0_conv_W1, L0_conv_b1, L0_conv_W2, L0_conv_b2)
    x = _L1_conv_ref(x, L1_conv_w_conv1_pw, L1_conv_b_conv1_pw, L1_conv_w_conv1_dw, L1_conv_b_conv1_dw, L1_conv_w_conv2_g, L1_conv_b_conv2_g, L1_conv_w_conv2_pw, L1_conv_b_conv2_pw, L1_conv_w_conv211, L1_conv_b_conv211, L1_conv_attgamma, L1_conv_ga1, L1_conv_selfb, L1_conv_selfw)
    return x


_drawn_inputs = setup_inputs


def setup_inputs(seed=0):
    import zlib

    import numpy as np

    out = dict(_drawn_inputs(seed))
    spreads = {'L0_conv_bq': (0.0, 0.433),
     'L0_conv_bk': (0.0, 2.0),
     'L0_conv_bv': (0.0, 0.1),
     'L0_conv_b1': (0.0, 0.1),
     'L0_conv_b2': (0.0, 0.1),
     'L1_conv_attgamma': (0.009999999776482582, 0.6),
     'L1_conv_ga1': (0.009999999776482582, 0.6)}
    factors = {'L1_conv_b_conv1_pw': 8.0,
     'L1_conv_w_conv2_g': 64.0,
     'L1_conv_b_conv2_g': 64.0,
     'L1_conv_w_conv2_pw': 64.0,
     'L1_conv_b_conv2_pw': 200.0,
     'L1_conv_w_conv211': 8.0,
     'L1_conv_b_conv211': 155.114,
     'L1_conv_selfb': 8.0,
     'L1_conv_selfw': 8.0}
    for name, (base, spread) in spreads.items():
        noise = np.random.default_rng([zlib.crc32(name.encode()), seed]).standard_normal(out[name].shape)
        drawn = base * np.exp(spread * noise) if base else spread * noise
        out[name] = jnp.asarray(drawn.astype(out[name].dtype))
    for name, factor in factors.items():
        out[name] = (out[name] * factor).astype(out[name].dtype)
    return out
```

```python
from contextlib import ExitStack

import concourse.bass as bass
from concourse import mybir

FP32 = mybir.dt.float32
FP32R = mybir.dt.float32r
ALU = mybir.AluOpType
ACT = mybir.ActivationFunctionType
AXIS_X = mybir.AxisListType.X

C = 128
H = W = 128
GS = 8
WIN = GS * GS
HID = 256
BANK = 512

TILES_PER_IMAGE = H // GS
PAIRS = W // GS // 2
HALF = W // 2
ROWS = 16
BANDS_PER_IMAGE = H // ROWS
PAD = 2
WP = W + 2
XROWS = ROWS + 4
EROWS = ROWS + 2
CHUNK_ROWS = BANK // W
CHUNKS = ROWS // CHUNK_ROWS
PW_CHUNKS = XROWS // CHUNK_ROWS
TAPS = 9
NSET = 16
Q = CHUNKS * TAPS
PRODUCTS = 4


def at_least(engine, semaphore, value):
    if isinstance(value, int) and value <= 0:
        return
    engine.wait_ge(semaphore, value)


def pipelined(engine, steps, step):
    step(0, None, 0)
    step(1, 0, 1)
    step(2, 1, 0)
    with engine.Fori(1, steps // 2 - 1) as i:
        step(i * 2 + 1, i * 2, 1)
        step(i * 2 + 2, i * 2 + 1, 0)
    step(steps - 1, steps - 2, 1)
    step(None, steps - 1, 0)


def window_pair(image_rows, pair):
    return image_rows[:, :, 2 * GS * pair:2 * GS * (pair + 1)].rearrange("c h (w v) -> c w h v", w=2)


def score_window(slot, half):
    group, odd = divmod(slot, 2)
    return 4 * group + ((3, 1) if odd else (0, 2))[half]


def windows(in_window_order):
    return in_window_order.rearrange("c w (h v) -> c w h v", v=GS)


def mix_tokens(nc, x, x2, Wq, bq, Wk, bk, Wv, bv, W1, b1, W2, b2):
    images = x.shape[0]
    tiles = images * TILES_PER_IMAGE
    scale = 1.0 / float(C) ** 0.5
    with ExitStack() as ctx:
        def sb(name, shape, dt=FP32):
            return ctx.enter_context(nc.sbuf_tensor(name, shape, dt))

        def bank(name, banks=1):
            return ctx.enter_context(nc.psum_tensor(name, [C, banks * BANK], FP32))

        def sem(name):
            return ctx.enter_context(nc.semaphore(name))

        raw = sb("raw", [C, 7, C])
        wT = sb("wT", [C, 7, C])
        ident = sb("ident", [C, C])
        bias_q, bias_k, bias_v, bias_2 = (sb(f"bias_{n}", [C, 1]) for n in "qkv2")
        bias_1 = sb("bias_1", [C, 2])
        zero_rows = sb("zero_rows", [C, images, PAD * W])
        xt = [sb(f"xt{p}", [C, GS, W]) for p in range(2)]
        xw = sb("xw", [C, 2 * PAIRS, WIN])
        q_sb = sb("q_sb", [C, 2 * PAIRS, WIN])
        k_sb = sb("k_sb", [C, 2 * PAIRS, WIN])
        vT = sb("vT", [C, PAIRS, C])
        row_max = sb("row_max", [C, PAIRS])
        row_sum = sb("row_sum", [C, PAIRS])
        row_inv = sb("row_inv", [C, PAIRS])
        scores = sb("scores", [C, PAIRS, WIN])
        expd = sb("expd", [C, PAIRS, WIN])
        probs = sb("probs", [C, PAIRS, WIN])
        probsT = sb("probsT", [C, PAIRS, C])
        x1 = sb("x1", [C, GS, W])
        hidden = sb("hidden", [C, 2, 2, BANK])
        xo = [sb(f"xo{p}", [C, GS, W]) for p in range(2)]

        ring = [bank(f"ring{p}") for p in range(2)]
        ps_s = bank("ps_s")
        ps_ta = bank("ps_ta", 2)
        ps_w2 = bank("ps_w2", 2)

        loaded = sem("loaded")
        ident_zero, ident_ready = sem("ident_zero"), sem("ident_ready")
        zeros_ready, zeros_stored = sem("zeros_ready"), sem("zeros_stored")
        wt_done, wt_ready = sem("wt_done"), sem("wt_ready")
        xw_ready = sem("xw_ready")
        x_in = [sem(f"x_in{p}") for p in range(2)]
        stored = [sem(f"stored{p}") for p in range(2)]
        qkv_done, qkv_ready = sem("qkv_done"), sem("qkv_ready")
        s_done, maxed, centred, exp_done = sem("s_done"), sem("maxed"), sem("centred"), sem("exp_done")
        summed, inverted, probs_ready = sem("summed"), sem("inverted"), sem("probs_ready")
        t_done, probsT_ready, av_done, x1_ready = sem("t_done"), sem("probsT_ready"), sem("av_done"), sem("x1_ready")
        w1_done, gelu_ready, w2_done, xo_ready = sem("w1_done"), sem("gelu_ready"), sem("w2_done"), sem("xo_ready")

        def input_count(m, p):
            return (m - p) // 2 * 16 + 16 if isinstance(m, int) else (m - p) * 8 + 16

        def half(t, h):
            return t[:, :, HALF * h:HALF * (h + 1)]

        def x_tile(n):
            first = (n % TILES_PER_IMAGE) * GS
            return x[bass.ds(n // TILES_PER_IMAGE, 1), :, bass.ds(first, GS), :].rearrange("b c h w -> (b c) h w")

        def x2_tile(n):
            first = (n % TILES_PER_IMAGE) * GS + PAD
            return x2[bass.ds(n // TILES_PER_IMAGE, 1), :, bass.ds(first, GS), :].rearrange("b c h w -> (b c) h w")

        with nc.Block() as block:
            @block.sync
            def _(sp):
                for i, w in enumerate((Wq, Wk, Wv, W1[0:C, :], W1[C:HID, :], W2[:, 0:C], W2[:, C:HID])):
                    sp.dma_start(raw[:, i, :], w).then_inc(loaded, 16)
                for t, b in ((bias_q, bq), (bias_k, bk), (bias_v, bv), (bias_2, b2)):
                    sp.dma_start(t[:, :], b.rearrange("(c a) -> c a", a=1)).then_inc(loaded, 16)
                for m in range(2):
                    sp.dma_start(bias_1[:, m:m + 1], b1[m * C:(m + 1) * C].rearrange("(c a) -> c a", a=1)).then_inc(loaded, 16)
                sp.dma_start(xt[0][:, :, :], x_tile(0)).then_inc(x_in[0], 16)
                sp.dma_start(xt[1][:, :, :], x_tile(1)).then_inc(x_in[1], 16)
                sp.wait_ge(zeros_ready, 1)
                for r in (0, H + PAD):
                    sp.dma_start(x2[:, :, r:r + PAD, :].rearrange("b c h w -> c b (h w)"), zero_rows[:, :, :]).then_inc(zeros_stored, 16)

                def load_and_store(n, p, uses, more=True):
                    if more:
                        sp.wait_ge(x1_ready, 2 * n + 2)
                        sp.dma_start(xt[p][:, :, :], x_tile(n + 2)).then_inc(x_in[p], 16)
                    sp.wait_ge(xo_ready, 2 * n + 2)
                    sp.dma_start(x2_tile(n), xo[p][:, :, :]).then_inc(stored[p], 16)

                with sp.Fori(0, tiles // 2 - 1) as i:
                    load_and_store(i * 2, 0, i)
                    load_and_store(i * 2 + 1, 1, i)
                load_and_store(tiles - 2, 0, None, more=False)
                load_and_store(tiles - 1, 1, None, more=False)
                for p in range(2):
                    sp.wait_ge(stored[p], 16 * (tiles // 2))
                sp.wait_ge(zeros_stored, 32)

            @block.gpsimd
            def _(pool):
                nc.gpsimd.memset(ident[:, :], 0.0).then_inc(ident_zero, 1)
                pool.wait_ge(ident_zero, 1)
                nc.gpsimd.affine_select(out=ident[:, :], in_=ident[:, :], compare_op=ALU.not_equal, fill=1.0, base=0,
                                        pattern=[[-1, C]], channel_multiplier=1).then_inc(ident_ready, 1)
                nc.gpsimd.memset(zero_rows[:, :, :], 0.0).then_inc(zeros_ready, 1)
                nc.gpsimd.memset(probsT[:, :, :], 0.0).then_inc(zeros_ready, 1)

            @block.tensor
            def _(pe):
                pe.wait_ge(loaded, 16 * 13)
                pe.wait_ge(ident_ready, 1)
                for i in range(7):
                    if i >= 2:
                        pe.wait_ge(wt_ready, i - 1)
                    nc.tensor.matmul(ring[i % 2][:, 0:C], raw[:, i, :], ident[:, :], is_transpose=True,
                                     start=True, stop=True).then_inc(wt_done, 1)
                pe.wait_ge(wt_ready, 7)

                def project(m, p, which):
                    if which == 0:
                        at_least(pe, x_in[p], input_count(m, p))
                    for h in range(2):
                        if which == 0:
                            at_least(pe, gelu_ready, 4 * m - 5 + h)
                        else:
                            pe.wait_ge(qkv_ready, 6 * m + 1 + h)
                        nc.tensor.matmul(ring[h][:, :], wT[:, which, :], half(xt[p], h), start=True, stop=True).then_inc(qkv_done, 1)

                def values(m, p):
                    pe.wait_ge(xw_ready, m + 1)
                    for h in range(2):
                        pe.wait_ge(qkv_ready, 6 * m + 3 + h)
                        for j in range(PAIRS // 2):
                            mm = nc.tensor.matmul(ring[h][:, C * j:C * (j + 1)], xw[:, PAIRS * h + 2 * j:PAIRS * h + 2 * j + 2, :], wT[:, 2, :],
                                                  start=(j == 0), stop=(j == PAIRS // 2 - 1), skip_group_check=True)
                        mm.then_inc(qkv_done, 1)

                def window_scores(m):
                    pe.wait_ge(qkv_ready, 6 * m + 4)
                    at_least(pe, centred, m)
                    for a in range(2):
                        for j in range(PAIRS):
                            w = score_window(j, a)
                            mm = nc.tensor.matmul(ps_s[WIN * a:WIN * (a + 1), WIN * j:WIN * (j + 1)],
                                                  q_sb[:, w, :], k_sb[:, w, :],
                                                  start=(j == 0), stop=(j == PAIRS - 1), skip_group_check=True)
                    mm.then_inc(s_done, 1)

                def transpose_probs(n):
                    pe.wait_ge(probs_ready, n + 1)
                    at_least(pe, x1_ready, 2 * n - 1)
                    for g in range(PAIRS // 2):
                        mm = nc.tensor.matmul(ps_ta[:, C * g:C * (g + 1)], probs[:, 2 * g:2 * g + 2, :], ident[:, :],
                                              is_transpose=True, start=True, stop=True)
                    mm.then_inc(t_done, 1)

                def attend(n):
                    pe.wait_ge(probsT_ready, n + 1)
                    pe.wait_ge(qkv_ready, 6 * n + 6)
                    for h in range(2):
                        out = ps_ta[:, BANK * h:BANK * (h + 1)].rearrange("c (h w) -> c h w", h=GS)
                        for j in range(PAIRS // 2):
                            pair = h * PAIRS // 2 + j
                            mm = nc.tensor.matmul(window_pair(out, j), vT[:, pair, :], probsT[:, pair, :],
                                                  start=(j == 0), stop=(j == PAIRS // 2 - 1), skip_group_check=True)
                        mm.then_inc(av_done, 1)

                def mlp_up(n, front):
                    pe.wait_ge(x1_ready, 2 * n + 2)
                    for h in range(2):
                        for m in range(2):
                            if h == 1:
                                pe.wait_ge(gelu_ready, 4 * n + 1 + m)
                            elif front:
                                pe.wait_ge(qkv_ready, 6 * n + 11 + m)
                            else:
                                pe.wait_ge(gelu_ready, 4 * n - 1 + m)
                            nc.tensor.matmul(ring[m][:, :], wT[:, 3 + m, :], x1[:, 4 * h:4 * h + 4, :],
                                             start=True, stop=True).then_inc(w1_done, 1)

                def mlp_down(n):
                    for h in range(2):
                        pe.wait_ge(gelu_ready, 4 * n + 2 + 2 * h)
                        at_least(pe, xo_ready, 2 * n - 1 + h)
                        for m in range(2):
                            mm = nc.tensor.matmul(ps_w2[:, BANK * h:BANK * (h + 1)], wT[:, 5 + m, :], hidden[:, h, m, :],
                                                  start=(m == 0), stop=(m == 1))
                        mm.then_inc(w2_done, 1)

                def step(m, n, p):
                    if n is not None:
                        transpose_probs(n)
                    if m is not None:
                        project(m, p, 0)
                        project(m, p, 1)
                    if n is not None:
                        attend(n)
                    if m is not None:
                        values(m, p)
                        window_scores(m)
                    if n is not None:
                        mlp_up(n, m is not None)
                        mlp_down(n)

                pipelined(pe, tiles, step)

            @block.scalar
            def _(act):
                act.wait_ge(loaded, 16 * 13)
                act.wait_ge(zeros_ready, 2)

                def step(m, n, p):
                    if n is not None:
                        act.wait_ge(t_done, n + 1)
                        at_least(act, av_done, 2 * n)
                        low = ps_ta[WIN:C, 0:BANK].rearrange("l (g b k) -> l g b k", b=2, k=WIN)
                        nc.scalar.activation(probsT[0:WIN, :, 0:WIN], ps_ta[0:WIN, 0:BANK].rearrange("l (j k) -> l j k", k=WIN), ACT.Copy)
                        for b in range(2):
                            a = nc.scalar.activation(probsT[WIN:C, b:PAIRS:2, WIN:C], low[:, :, 1 - b, :], ACT.Copy)
                        a.then_inc(probsT_ready, 1)
                    if m is not None:
                        at_least(act, s_done, m)
                        for i, (dst, bias) in enumerate(((q_sb, bias_q), (k_sb, bias_k))):
                            for h in range(2):
                                act.wait_ge(qkv_done, 6 * m + 2 * i + h + 1)
                                nc.scalar.activation(windows(dst[:, PAIRS * h:PAIRS * (h + 1), :]),
                                                     ring[h][:, :].rearrange("c (h w v) -> c w h v", h=GS, v=GS),
                                                     ACT.Identity, bias=bias[:, 0:1]).then_inc(qkv_ready, 1)
                        at_least(act, av_done, 2 * m)
                        for h in range(2):
                            act.wait_ge(qkv_done, 6 * m + 5 + h)
                            nc.scalar.activation(vT[:, 4 * h:4 * h + 4, :], ring[h][:, :].rearrange("c (h w) -> c h w", h=4),
                                                 ACT.Copy).then_inc(qkv_ready, 1)
                        act.wait_ge(centred, m + 1)
                        at_least(act, probs_ready, m)
                        nc.scalar.activation(expd[:, :, :], scores[:, :, :], ACT.Exp, scale=scale).then_inc(exp_done, 1)
                    if n is not None:
                        at_least(act, w2_done, 2 * n)
                        for h in range(2):
                            for i in range(2):
                                act.wait_ge(w1_done, 4 * n + 2 * h + i + 1)
                                nc.scalar.activation(hidden[:, h, i, :], ring[i][:, :], ACT.Gelu,
                                                     bias=bias_1[:, i:i + 1]).then_inc(gelu_ready, 1)

                pipelined(act, tiles, step)

            @block.vector
            def _(dve):
                for i in range(7):
                    dve.wait_ge(wt_done, i + 1)
                    nc.vector.tensor_copy(wT[:, i, :], ring[i % 2][:, 0:C]).then_inc(wt_ready, 1)

                def stores_done(n, p):
                    if isinstance(n, int):
                        at_least(dve, stored[p], (n - p) // 2 * 16)
                    else:
                        dve.wait_ge(stored[p], (n - p) * 8)

                def step(m, n, p):
                    if m is not None:
                        dve.wait_ge(x_in[p], input_count(m, p))
                        at_least(dve, qkv_done, 6 * m)
                        nc.vector.tensor_copy(windows(xw[:, :, :]), xt[p][:, :, :].rearrange("c h (w v) -> c w h v", v=GS)).then_inc(xw_ready, 1)
                    if n is not None:
                        at_least(dve, w1_done, 4 * n)
                        at_least(dve, xo_ready, 2 * n)
                        for h in range(2):
                            dve.wait_ge(av_done, 2 * n + h + 1)
                            nc.vector.scalar_tensor_tensor(
                                out=half(x1, h), in0=ps_ta[:, BANK * h:BANK * (h + 1)].rearrange("c (h w) -> c h w", h=GS),
                                scalar=bias_v[:, 0:1], in1=half(xt[1 - p], h), op0=ALU.add, op1=ALU.add).then_inc(x1_ready, 1)
                    if m is not None:
                        s = ps_s[:, :].rearrange("k (j l) -> k j l", l=WIN)
                        dve.wait_ge(s_done, m + 1)
                        nc.vector.reduce_max(row_max[:, :], s, AXIS_X).then_inc(maxed, 1)
                        dve.wait_ge(maxed, m + 1)
                        at_least(dve, exp_done, m)
                        nc.vector.tensor_tensor(scores[:, :, :], s, row_max[:, :].unsqueeze(2).to_broadcast([C, PAIRS, WIN]),
                                                ALU.subtract).then_inc(centred, 1)
                        dve.wait_ge(exp_done, m + 1)
                        nc.vector.reduce_sum(row_sum[:, :], expd[:, :, :], AXIS_X).then_inc(summed, 1)
                        dve.wait_ge(summed, m + 1)
                        nc.vector.reciprocal(row_inv[:, :], row_sum[:, :]).then_inc(inverted, 1)
                        dve.wait_ge(inverted, m + 1)
                        at_least(dve, t_done, m)
                        nc.vector.tensor_tensor(probs[:, :, :], expd[:, :, :], row_inv[:, :].unsqueeze(2).to_broadcast([C, PAIRS, WIN]),
                                                ALU.mult).then_inc(probs_ready, 1)
                    if n is not None:
                        stores_done(n, 1 - p)
                        for h in range(2):
                            dve.wait_ge(w2_done, 2 * n + h + 1)
                            nc.vector.scalar_tensor_tensor(
                                out=xo[1 - p][:, 4 * h:4 * h + 4, :], in0=ps_w2[:, BANK * h:BANK * (h + 1)].rearrange("c (h w) -> c h w", w=W),
                                scalar=bias_2[:, 0:1], in1=x1[:, 4 * h:4 * h + 4, :], op0=ALU.add, op1=ALU.add).then_inc(xo_ready, 1)

                pipelined(dve, tiles, step)


def convolve(nc, x2, out, w_pw, b_pw, w_dw, b_dw, w_g, b_g, w_att, b_att, w_211, b_211, gamma, ga1, selfb, selfw):
    images = out.shape[0]
    bands = images * BANDS_PER_IMAGE
    SLOTS = 2 * TAPS + 1
    with ExitStack() as ctx:
        ctx.enter_context(nc.allow_non_contiguous_dma(reason="small transposed weights"))

        def sb(name, shape, dt=FP32):
            return ctx.enter_context(nc.sbuf_tensor(name, shape, dt))

        def bank(name, banks=1):
            return ctx.enter_context(nc.psum_tensor(name, [C, banks * BANK], FP32))

        def sem(name):
            return ctx.enter_context(nc.semaphore(name))

        ident = sb("ident2", [C, C])
        pw_raw = sb("pw_raw", [C, C])
        pwT = sb("pwT", [C, C])
        bias_pw, bias_dw = sb("bias_pw", [C, 1]), sb("bias_dw", [C, 1])
        dw = sb("dw", [C, TAPS])
        g_raw = sb("g_raw", [C, TAPS])
        g_mask = sb("g_mask", [C, NSET])
        gT = sb("gT", [C, TAPS, 32])
        bias_h = sb("bias_h", [C, 1])
        att_raw = sb("att_raw", [C, CHUNKS, 32])
        att_gamma = sb("att_gamma", [C, CHUNKS, 32])
        attA = sb("attA", [C, CHUNKS, 32])
        attB = sb("attB", [C, CHUNKS, 32])
        gamma_col, b_att_col, bias_att = sb("gamma_col", [C, 1]), sb("b_att_col", [C, 1]), sb("bias_att", [C, 1])
        sw_raw = sb("sw_raw", [C, 2 * TAPS * C])
        sb_raw = sb("sb_raw", [C, C])
        ga_row = sb("ga_row", [C, C])
        basis_full = sb("basis_full", [C, SLOTS, C])
        basis = sb("basis", [C, SLOTS, C], FP32R)
        flag_top, flag_bottom = sb("flag_top", [C, bands]), sb("flag_bottom", [C, bands])
        bias_top, bias_bottom = sb("bias_top", [C, bands]), sb("bias_bottom", [C, bands])

        xin = [sb(f"xin{p}", [C, XROWS, WP]) for p in range(2)]
        e0 = sb("e0", [C, XROWS, WP])
        enh = [sb(f"enh{p}", [C, 2, EROWS, WP]) for p in range(2)]
        enh_x = [sb(f"enh_x{p}", [C, ROWS, W]) for p in range(2)]
        h_sb = sb("h_sb", [C, BANK])
        h_up = sb("h_up", [C, BANK])
        h_prod = sb("h_prod", [C, BANK])
        att_hi = sb("att_hi", [C, BANK], FP32R)
        att_lo = sb("att_lo", [C, BANK], FP32R)
        att = [sb(f"att{p}", [C, CHUNKS, BANK], FP32R) for p in range(2)]
        products = [sb(f"products{i}", [C, 2, BANK]) for i in range(PRODUCTS)]
        summedT = [sb(f"summedT{i}", [C, BANK]) for i in range(2)]
        out_sb = [sb(f"out_sb{p}", [C, ROWS, W]) for p in range(2)]

        ps_k = [bank(f"ps_k{i}", 2) for i in range(2)]
        ps_t = [bank(f"ps_t{i}") for i in range(2)]
        ps_f = bank("ps_f")
        ps_m = bank("ps_m")

        loaded, zeroed, ident_ready = sem("loaded2"), sem("zeroed"), sem("ident_ready2")
        mask_step, setup_step, pwT_done, basis_ready = sem("mask_step"), sem("setup_step"), sem("pwT_done"), sem("basis_ready")
        flags_ready = sem("flags_ready")
        x_in = [sem(f"band_in{p}") for p in range(2)]
        pw_done, e0_ready = sem("pw_done"), sem("e0_ready")
        conv_done, h_ready, moved, h_prod_ready = sem("conv_done"), sem("h_ready"), sem("moved"), sem("h_prod_ready")
        att_done, att_hi_ready, att_lo_ready = sem("att_done"), sem("att_hi_ready"), sem("att_lo_ready")
        att_in = [sem(f"att_in{p}") for p in range(2)]
        dw_done, enh_ready, enh_x_ready = sem("dw_done"), sem("enh_ready"), sem("enh_x_ready")
        swapped = [sem(f"swapped{p}") for p in range(2)]
        k_done, product_ready, term_done = sem("k_done"), sem("product_ready"), sem("term_done")
        sum_done, sumT_ready, back_done, out_ready = sem("sum_done"), sem("sumT_ready"), sem("back_done"), sem("out_ready")
        stored = [sem(f"band_stored{p}") for p in range(2)]

        LOADS = 7 + CHUNKS * 5 + CHUNKS + 4 * 2
        DW_PIECES = 2 * TAPS
        DW_ROWS = EROWS // 2

        def rounds(n, p, each):
            return (n - p) // 2 * each if isinstance(n, int) else (n - p) * (each // 2)

        def x_band(n):
            return x2[bass.ds(n // BANDS_PER_IMAGE, 1), :, bass.ds((n % BANDS_PER_IMAGE) * ROWS, XROWS), :].rearrange("b c h w -> (b c) h w")

        def out_band(n):
            return out[bass.ds(n // BANDS_PER_IMAGE, 1), :, bass.ds((n % BANDS_PER_IMAGE) * ROWS, ROWS), :].rearrange("b c h w -> (b c) h w")

        with nc.Block() as block:
            @block.sync
            def _(sp):
                sp.wait_ge(zeroed, 1)
                count = [0]

                def load(dst, src):
                    sp.dma_start(dst, src).then_inc(loaded, 16)
                    count[0] += 1

                def column(v):
                    return v.rearrange("(c a) -> c a", a=1)

                load(pw_raw[:, :], w_pw.rearrange("o c a b -> o (c a b)"))
                load(bias_pw[:, :], column(b_pw))
                load(bias_dw[:, :], column(b_dw))
                load(dw[:, :], w_dw.rearrange("c a h w -> c (a h w)"))
                load(g_raw[:, :], w_g.rearrange("o i h w -> (o i) (h w)"))
                load(gT[:, TAPS // 2, NSET:2 * NSET], w_211.rearrange("n c a b -> c (n a b)"))
                load(ga_row[:, :], ga1.rearrange("a c b d -> a (c b d)").to_broadcast([C, C]))
                for j in range(CHUNKS):
                    r = 32 * j
                    load(bias_h[r:r + NSET, :], column(b_g))
                    load(bias_h[r + NSET:r + 2 * NSET, :], column(b_211))
                    load(gamma_col[r:r + NSET, :], column(gamma.rearrange("a n b c -> (a n b c)")))
                    load(b_att_col[r:r + NSET, :], column(b_att))
                    load(att_raw[r:r + NSET // 2, j, 0:NSET], w_att.rearrange("n k a b -> k (n a b)"))
                for j in range(CHUNKS):
                    load(att_gamma[:, j, 0:NSET], gamma.rearrange("a n b c -> a (n b c)").to_broadcast([C, NSET]))
                for j in range(4):
                    load(sw_raw[32 * j:32 * j + NSET, :], selfw[0])
                    load(sb_raw[32 * j:32 * j + NSET, :], selfb[0])
                assert count[0] == LOADS, count[0]

                def swap_channels(m, p):
                    sp.wait_ge(enh_ready, 2 * m + 2)
                    for i in range(2):
                        sp.dma_start(enh[p][i:C:2, 1, :, :], enh[p][1 - i:C:2, 0, :, :]).then_inc(swapped[p], 16)

                def loads(m, p):
                    at_least(sp, enh_x_ready, m - 1)
                    sp.dma_start(xin[p][:, :, 1:W + 1], x_band(m)).then_inc(x_in[p], 16)

                def attention_rows(m, p):
                    sp.wait_ge(att_hi_ready, m + 1)
                    for block_row, src in ((0, att_hi), (1, att_hi), (2, att_lo), (3, att_lo)):
                        if block_row == 2:
                            sp.wait_ge(att_lo_ready, m + 1)
                        for j in range(CHUNKS):
                            sp.dma_start(att[p][32 * block_row:32 * block_row + NSET, j, :].bitcast(FP32),
                                         src[32 * j:32 * j + NSET, :].bitcast(FP32)).then_inc(att_in[p], 16)

                loads(0, 0)
                loads(1, 1)

                def full_step(m, p):
                    attention_rows(m, p)
                    swap_channels(m, p)
                    if not isinstance(m, int) or m + 2 < bands:
                        loads(m + 2, p)

                full_step(0, 0)
                full_step(1, 1)
                with sp.Fori(1, bands // 2 - 1) as i:
                    full_step(i * 2, 0)
                    full_step(i * 2 + 1, 1)
                full_step(bands - 2, 0)
                full_step(bands - 1, 1)

            @block.gpsimd
            def _(pool):
                for t in (bias_h, gamma_col, b_att_col, sb_raw):
                    nc.gpsimd.memset(t[:, :], 0.0)
                for t in (att_raw, att_gamma, attB, gT):
                    nc.gpsimd.memset(t[:, :, :], 0.0)
                nc.gpsimd.memset(sw_raw[:, :], 0.0)
                for p in range(2):
                    nc.gpsimd.memset(xin[p][:, :, :], 0.0)
                    nc.gpsimd.memset(enh[p][:, :, :, :], 0.0)
                    nc.gpsimd.memset(att[p][:, :, :].bitcast(FP32), 0.0)
                nc.gpsimd.memset(e0[:, :, :], 0.0)
                for t in (flag_top, flag_bottom):
                    nc.gpsimd.memset(t[:, :], 1.0)
                nc.gpsimd.memset(g_mask[:, :], 1.0)
                nc.gpsimd.memset(ident[:, :], 0.0).then_inc(zeroed, 1)
                pool.wait_ge(zeroed, 1)
                nc.gpsimd.affine_select(out=ident[:, :], in_=ident[:, :], compare_op=ALU.not_equal, fill=1.0, base=0,
                                        pattern=[[-1, C]], channel_multiplier=1).then_inc(ident_ready, 1)
                nc.gpsimd.affine_select(out=g_mask[:, :], in_=g_mask[:, :], compare_op=ALU.is_ge, fill=0.0, base=0,
                                        pattern=[[-8, NSET]], channel_multiplier=1).then_inc(mask_step, 1)
                pool.wait_ge(mask_step, 1)
                nc.gpsimd.affine_select(out=g_mask[:, :], in_=g_mask[:, :], compare_op=ALU.is_ge, fill=0.0, base=7,
                                        pattern=[[8, NSET]], channel_multiplier=-1).then_inc(mask_step, 1)
                nc.gpsimd.affine_select(out=attB[:, :, 0:NSET], in_=attB[:, :, 0:NSET], compare_op=ALU.not_equal, fill=1.0,
                                        base=-NSET, pattern=[[-32, CHUNKS], [-1, NSET]], channel_multiplier=1).then_inc(mask_step, 1)
                nc.gpsimd.memset(flag_top[:, :].rearrange("c (b k) -> c b k", k=BANDS_PER_IMAGE)[:, :, 0:1], 0.0)
                nc.gpsimd.memset(flag_bottom[:, :].rearrange("c (b k) -> c b k", k=BANDS_PER_IMAGE)[:, :, BANDS_PER_IMAGE - 1:BANDS_PER_IMAGE],
                                 0.0).then_inc(mask_step, 1)

                def step(m, n, p):
                    if m is not None:
                        pool.wait_ge(enh_ready, 2 * m + 2)
                        at_least(pool, sum_done, CHUNKS * (m - 1))
                        nc.gpsimd.tensor_tensor(enh_x[p][:, :, :], enh[p][:, 0, 1:ROWS + 1, 1:W + 1],
                                                xin[p][:, 2:ROWS + 2, 1:W + 1], ALU.add).then_inc(enh_x_ready, 1)
                    if n is not None:
                        pool.wait_ge(out_ready, CHUNKS * n + CHUNKS)
                        pool.dma_start(out_band(n), out_sb[1 - p][:, :, :]).then_inc(stored[1 - p], 16)

                pipelined(pool, bands, step)
                for p in range(2):
                    pool.wait_ge(stored[p], 16 * (bands // 2))

            @block.tensor
            def _(pe):
                pe.wait_ge(loaded, 16 * (LOADS))
                pe.wait_ge(ident_ready, 1)
                nc.tensor.matmul(ps_m[:, 0:C], pw_raw[:, :], ident[:, :], is_transpose=True, start=True, stop=True).then_inc(pwT_done, 1)
                pe.wait_ge(basis_ready, 1)

                def pointwise(m, p, c):
                    if c == 0:
                        pe.wait_ge(x_in[p], rounds(m, p, 16) + 16)
                        at_least(pe, att_lo_ready, m)
                    else:
                        pe.wait_ge(e0_ready, PW_CHUNKS * m + c)
                    nc.tensor.matmul(ps_m[:, :], pwT[:, :], xin[p][:, CHUNK_ROWS * c:CHUNK_ROWS * (c + 1), 1:W + 1],
                                     start=True, stop=True).then_inc(pw_done, 1)

                def group_tap(m, p, t):
                    if t == 0:
                        pe.wait_ge(e0_ready, PW_CHUNKS * m + PW_CHUNKS)
                    dy, dx = divmod(t, 3)
                    for j in range(CHUNKS):
                        r = 1 + CHUNK_ROWS * j + dy
                        mm = nc.tensor.matmul(ps_m[32 * j:32 * j + 32, :], gT[:, t, :], xin[p][:, r:r + CHUNK_ROWS, dx:dx + W],
                                              start=(t == 0), stop=(t == TAPS - 1))
                    if t == TAPS - 1:
                        mm.then_inc(conv_done, 1)

                def coefficients(m):
                    pe.wait_ge(h_prod_ready, m + 1)
                    nc.tensor.matmul(ps_m[:, :], attA[:, :, :], h_prod[:, :], start=True, stop=False)
                    nc.tensor.matmul(ps_m[:, :], attB[:, :, :], h_sb[:, :], start=False, stop=True).then_inc(att_done, 1)

                def basis_kernels(n, p, q):
                    j, t = divmod(q, TAPS)
                    at_least(pe, product_ready, Q * n + q - 1)
                    for s in range(2):
                        mm = nc.tensor.matmul(ps_k[q % 2][:, BANK * s:BANK * (s + 1)], basis[:, 2 * t + s, :], att[p][:, j, :],
                                              start=True, stop=True)
                    mm.then_inc(k_done, 1)

                def add_products(n, p, q):
                    j, t = divmod(q, TAPS)
                    pe.wait_ge(product_ready, Q * n + q + 1)
                    if t == 0:
                        at_least(pe, sumT_ready, CHUNKS * n + j - 1)
                    for s in range(2):
                        for r in range(CHUNK_ROWS):
                            mm = nc.tensor.matmul(ps_t[j % 2][:, C * r:C * (r + 1)], products[q % PRODUCTS][:, s, C * r:C * (r + 1)],
                                                  ident[:, :], is_transpose=True, start=(t == 0 and s == 0 and r == 0), stop=False,
                                                  skip_group_check=True)
                    mm.then_inc(term_done, 1)
                    if t == TAPS - 1:
                        for r in range(CHUNK_ROWS):
                            mm = nc.tensor.matmul(ps_t[j % 2][:, C * r:C * (r + 1)], enh_x[p][:, CHUNK_ROWS * j + r, :], ident[:, :],
                                                  is_transpose=True, start=False, stop=(r == CHUNK_ROWS - 1), skip_group_check=True)
                        mm.then_inc(sum_done, 1)

                def back(n, p, j):
                    at_least(pe, out_ready, CHUNKS * n + j)
                    nc.tensor.matmul(ps_f[:, :], basis[:, SLOTS - 1, :], att[p][:, j, :], start=True, stop=False, skip_group_check=True)
                    pe.wait_ge(sumT_ready, CHUNKS * n + j + 1)
                    for r in range(CHUNK_ROWS):
                        mm = nc.tensor.matmul(ps_f[:, C * r:C * (r + 1)], summedT[j % 2][:, C * r:C * (r + 1)], ident[:, :],
                                              is_transpose=True, start=False, stop=(r == CHUNK_ROWS - 1), skip_group_check=True)
                    mm.then_inc(back_done, 1)

                def step(m, n, p):
                    if n is not None:
                        b = 1 - p
                        pe.wait_ge(att_in[b], rounds(n, b, 256) + 256)
                        pe.wait_ge(enh_x_ready, n + 1)
                        basis_kernels(n, b, 0)
                        basis_kernels(n, b, 1)
                    for q in range(Q):
                        if n is not None:
                            add_products(n, b, q)
                            if q + 2 < Q:
                                basis_kernels(n, b, q + 2)
                        if m is not None:
                            if q in (1, 3, 5, 7, 9):
                                pointwise(m, p, (q - 1) // 2)
                            if 11 <= q < 11 + TAPS:
                                group_tap(m, p, q - 11)
                            if q == 25:
                                coefficients(m)
                        if n is not None and q in (10, 19, 28):
                            back(n, b, q // TAPS - 1)
                    if n is not None:
                        back(n, b, CHUNKS - 1)

                pipelined(pe, bands, step)

            @block.scalar
            def _(act):
                act.wait_ge(flags_ready, 1)

                def e0_rows(m, c):
                    act.wait_ge(pw_done, PW_CHUNKS * m + c + 1)
                    if c == 0:
                        at_least(act, dw_done, DW_PIECES * m)
                    ps = ps_m[:, :].rearrange("c (h w) -> c h w", w=W)
                    pieces = [(0, 4, bias_pw[:, 0:1])]
                    if c == 0:
                        pieces = [(0, 2, bias_top[:, bass.ds(m, 1)]), (2, 4, bias_pw[:, 0:1])]
                    if c == PW_CHUNKS - 1:
                        pieces = [(0, 2, bias_pw[:, 0:1]), (2, 4, bias_bottom[:, bass.ds(m, 1)])]
                    for lo, hi, bias in pieces:
                        a = nc.scalar.activation(e0[:, CHUNK_ROWS * c + lo:CHUNK_ROWS * c + hi, 1:W + 1], ps[:, lo:hi, :],
                                                 ACT.Identity, bias=bias)
                    a.then_inc(e0_ready, 1)

                def h_rows(m):
                    act.wait_ge(conv_done, m + 1)
                    nc.scalar.activation(h_sb[:, :], ps_m[:, :], ACT.Identity, bias=bias_h[:, 0:1]).then_inc(h_ready, 1)

                def att_high(m, p):
                    act.wait_ge(att_done, m + 1)
                    if isinstance(m, int) and m == 0:
                        pass
                    else:
                        act.wait_ge(att_in[1 - p], rounds(m - 1, 1 - p, 256) + 256)
                    nc.scalar.activation(att_hi[:, :], ps_m[:, :], ACT.Identity, bias=bias_att[:, 0:1]).then_inc(att_hi_ready, 1)

                def clear_outside(m, p):
                    act.wait_ge(dw_done, DW_PIECES * m + DW_PIECES)
                    for row, flag in ((0, flag_top), (EROWS - 1, flag_bottom)):
                        nc.scalar.activation(enh[p][:, 0, row, 1:W + 1], enh[p][:, 0, row, 1:W + 1], ACT.Copy,
                                             scale=flag[:, bass.ds(m, 1)]).then_inc(enh_ready, 1)

                def sum_out(n, j):
                    act.wait_ge(sum_done, CHUNKS * n + j + 1)
                    at_least(act, back_done, CHUNKS * n + j - 1)
                    nc.scalar.activation(summedT[j % 2][:, :], ps_t[j % 2][:, :], ACT.Copy).then_inc(sumT_ready, 1)

                def chunk_out(n, p, j):
                    act.wait_ge(back_done, CHUNKS * n + j + 1)
                    if j == 0:
                        at_least(act, stored[p], rounds(n, p, 16))
                    nc.scalar.activation(out_sb[p][:, CHUNK_ROWS * j:CHUNK_ROWS * (j + 1), :],
                                         ps_f[:, :].rearrange("c (h w) -> c h w", w=W), ACT.Copy).then_inc(out_ready, 1)

                def step(m, n, p):
                    if m is not None:
                        for c in range(4):
                            e0_rows(m, c)
                    if n is not None:
                        sum_out(n, 0)
                    if m is not None:
                        e0_rows(m, 4)
                    if n is not None:
                        chunk_out(n, 1 - p, 0)
                        sum_out(n, 1)
                    if m is not None and n is None:
                        h_rows(m)
                    if n is not None:
                        if m is not None:
                            h_rows(m)
                        chunk_out(n, 1 - p, 1)
                    if m is not None:
                        att_high(m, p)
                    if n is not None:
                        sum_out(n, 2)
                        chunk_out(n, 1 - p, 2)
                    if m is not None:
                        clear_outside(m, p)
                    if n is not None:
                        sum_out(n, 3)
                        chunk_out(n, 1 - p, 3)

                pipelined(act, bands, step)

            @block.vector
            def _(dve):
                dve.wait_ge(loaded, 16 * (LOADS))
                dve.wait_ge(mask_step, 4)
                for t in range(TAPS):
                    nc.vector.tensor_scalar(gT[:, t, 0:NSET], g_mask[:, :], g_raw[:, t:t + 1], None, ALU.mult)
                nc.vector.tensor_tensor(attA[:, :, :], att_raw[:, :, :], att_gamma[:, :, :], ALU.mult)
                nc.vector.tensor_tensor(bias_att[:, :], gamma_col[:, :], b_att_col[:, :], ALU.mult)
                nc.vector.tensor_scalar(bias_top[:, :], flag_top[:, :], bias_pw[:, 0:1], None, ALU.mult)
                nc.vector.tensor_scalar(bias_bottom[:, :], flag_bottom[:, :], bias_pw[:, 0:1], None, ALU.mult).then_inc(flags_ready, 1)
                ga = ga_row[:, :].rearrange("n (g i) -> n g i", i=2)
                by_group = sw_raw[:, :].rearrange("n (g m) -> n g m", m=4 * TAPS)
                for t in range(TAPS):
                    for i in range(2):
                        for s in range(2):
                            col = 2 * TAPS * i + TAPS * (i ^ s) + t
                            nc.vector.tensor_tensor(basis_full[:, 2 * t + s, :].rearrange("n (g i) -> n g i", i=2)[:, :, i:i + 1],
                                                    by_group[:, :, col:col + 1], ga[:, :, i:i + 1], ALU.mult)
                nc.vector.tensor_tensor(basis_full[:, SLOTS - 1, :], sb_raw[:, :], ga_row[:, :], ALU.mult).then_inc(setup_step, 1)
                dve.wait_ge(setup_step, 1)
                nc.vector.tensor_copy(basis[:, :, :], basis_full[:, :, :]).then_inc(setup_step, 1)
                dve.wait_ge(setup_step, 2)
                for r in (32, 96):
                    nc.vector.tensor_tensor(basis[r:r + 32, :, :], basis_full[r:r + 32, :, :], basis[r:r + 32, :, :].bitcast(FP32),
                                            ALU.subtract)
                dve.wait_ge(pwT_done, 1)
                nc.vector.tensor_copy(pwT[:, :], ps_m[:, 0:C]).then_inc(basis_ready, 1)

                def dw_piece(m, p, i):
                    t, half = divmod(i, 2)
                    dy, dx = divmod(t, 3)
                    r = DW_ROWS * half
                    src = e0[:, r + dy:r + dy + DW_ROWS, dx:dx + W]
                    dst = enh[p][:, 0, r:r + DW_ROWS, 1:W + 1]
                    if i == 0:
                        dve.wait_ge(e0_ready, PW_CHUNKS * m + PW_CHUNKS)
                        at_least(dve, enh_x_ready, m - 1)
                        at_least(dve, product_ready, Q * (m - 1))
                    if t == 0:
                        nc.vector.tensor_scalar(dst, src, dw[:, 0:1], bias_dw[:, 0:1], ALU.mult, ALU.add).then_inc(dw_done, 1)
                    else:
                        dve.wait_ge(dw_done, DW_PIECES * m + i - 1)
                        nc.vector.scalar_tensor_tensor(out=dst, in0=src, scalar=dw[:, t:t + 1], in1=dst,
                                                       op0=ALU.mult, op1=ALU.add).then_inc(dw_done, 1)

                def product(n, p, q):
                    j, t = divmod(q, TAPS)
                    dy, dx = divmod(t, 3)
                    r = CHUNK_ROWS * j + dy
                    dve.wait_ge(k_done, Q * n + q + 1)
                    at_least(dve, term_done, Q * n + q + 1 - PRODUCTS)
                    nc.vector.tensor_tensor(products[q % PRODUCTS][:, :, :].rearrange("c s (h w) -> c s h w", w=W),
                                            ps_k[q % 2][:, :].rearrange("c (s h w) -> c s h w", s=2, w=W),
                                            enh[p][:, :, r:r + CHUNK_ROWS, dx:dx + W], ALU.mult).then_inc(product_ready, 1)

                def step(m, n, p):
                    b = 1 - p
                    if n is not None:
                        dve.wait_ge(swapped[b], rounds(n, b, 32) + 32)
                    for q in range(Q):
                        if m is not None and q == 21:
                            dve.wait_ge(h_ready, m + 1)
                        if n is not None:
                            product(n, b, q)
                        if m is not None:
                            if 13 <= q < 13 + DW_PIECES:
                                dw_piece(m, p, q - 13)
                            if q == 21:
                                nc.vector.stream_shuffle(h_up[:, :], h_sb[:, :],
                                                         [(i + NSET // 2) % 32 for i in range(32)]).then_inc(moved, 1)
                            if q == 22:
                                dve.wait_ge(moved, m + 1)
                                nc.vector.tensor_tensor(h_prod[:, :], h_sb[:, :], h_up[:, :], ALU.mult).then_inc(h_prod_ready, 1)
                            if q == 28:
                                dve.wait_ge(att_hi_ready, m + 1)
                                nc.vector.scalar_tensor_tensor(out=att_lo[:, :], in0=ps_m[:, :], scalar=bias_att[:, 0:1],
                                                               in1=att_hi[:, :].bitcast(FP32), op0=ALU.add,
                                                               op1=ALU.subtract).then_inc(att_lo_ready, 1)

                pipelined(dve, bands, step)


def build(nc, x, Wq, bq, Wk, bk, Wv, bv, W1, b1, W2, b2, w_pw, b_pw, w_dw, b_dw, w_g, b_g, w_att, b_att,
          w_211, b_211, gamma, ga1, selfb, selfw, out):
    scratch = nc.dram_tensor("layer0_out", (x.shape[0], C, H + 2 * PAD, W), FP32, kind="Internal").ap()
    mix_tokens(nc, x, scratch, Wq, bq, Wk, bk, Wv, bv, W1, b1, W2, b2)
    convolve(nc, scratch, out, w_pw, b_pw, w_dw, b_dw, w_g, b_g, w_att, b_att, w_211, b_211, gamma, ga1, selfb, selfw)


_INPUTS = ["x", "L0_conv_Wq", "L0_conv_bq", "L0_conv_Wk", "L0_conv_bk", "L0_conv_Wv", "L0_conv_bv", "L0_conv_W1",
           "L0_conv_b1", "L0_conv_W2", "L0_conv_b2", "L1_conv_w_conv1_pw", "L1_conv_b_conv1_pw", "L1_conv_w_conv1_dw",
           "L1_conv_b_conv1_dw", "L1_conv_w_conv2_g", "L1_conv_b_conv2_g", "L1_conv_w_conv2_pw", "L1_conv_b_conv2_pw",
           "L1_conv_w_conv211", "L1_conv_b_conv211", "L1_conv_attgamma", "L1_conv_ga1", "L1_conv_selfb", "L1_conv_selfw"]


def kernel(**inputs):
    import numpy as np
    import concourse.bacc as bacc
    from concourse.bass_utils import run_bass_kernel_spmd

    nc = bacc.Bacc("TRN2", target_bir_lowering=False, num_devices=1)
    arrays, args = {}, []
    for name in _INPUTS:
        a = np.ascontiguousarray(inputs[name])
        arrays[f"in_{name}"] = a
        args.append(nc.dram_tensor(f"in_{name}", a.shape, mybir.dt.from_np(a.dtype), kind="ExternalInput").ap())
    out = nc.dram_tensor("out", inputs["x"].shape, FP32, kind="ExternalOutput").ap()
    build(nc, *args, out)
    r = run_bass_kernel_spmd(nc, [arrays], core_ids=[0])
    return r.results[0]["out"]
```

```python
from contextlib import ExitStack

import concourse.bass as bass
from concourse import mybir

FP32 = mybir.dt.float32
FP32R = mybir.dt.float32r
ALU = mybir.AluOpType
ACT = mybir.ActivationFunctionType
AXIS_X = mybir.AxisListType.X

C = 128
H = W = 128
GS = 8
WIN = GS * GS
HID = 256
BANK = 512

TILES_PER_IMAGE = H // GS
PAIRS = W // GS // 2
HALF = W // 2
ROWS = 16
BANDS_PER_IMAGE = H // ROWS
PAD = 2
WP = W + 2
XROWS = ROWS + 4
EROWS = ROWS + 2
CHUNK_ROWS = BANK // W
CHUNKS = ROWS // CHUNK_ROWS
PW_CHUNKS = XROWS // CHUNK_ROWS
TAPS = 9
NSET = 16
Q = CHUNKS * TAPS
PRODUCTS = 6
MERGED = (0, 3, 6)


def product_schedule():
    order, terms = [], []
    for q in range(Q):
        order.append(("product", q))
        for lead in (q - 2, q - 1) if q == Q - 1 or (q + 1) % TAPS == 0 else (q - 2,):
            if lead >= 0 and lead % TAPS in MERGED and ("merge", lead) not in order and lead + 1 <= q:
                order.append(("merge", lead))
    for q in range(Q):
        if q % TAPS in MERGED:
            terms.append(("merge", q))
        elif (q - 1) % TAPS not in MERGED or q % TAPS == 0:
            terms.append(("product", q))
    return order, terms


OPS, TERMS = product_schedule()
OP_COUNT = {op: i + 1 for i, op in enumerate(OPS)}
LAST_TERM = [[term for term in TERMS if term[1] // TAPS == j][-1] for j in range(CHUNKS)]
TERM_SLOT = {term: min([q for q in range(Q) if OP_COUNT["product", q] > OP_COUNT[term]] + [Q]) for term in TERMS}
BACK_SLOTS = [TAPS * j + TAPS + 5 for j in range(CHUNKS - 1)]
CONV_SLOTS = 18
COEFFICIENT_SLOT = 21
PW_SLOTS = [25, 27, 29, 31, 33]
MERGE_SLOT = {q: max(at for op, at in OPS[:OP_COUNT[kind, q]] if op == "product") for kind, q in OPS if kind == "merge"}
TERM_OF = {q: i for i, (kind, q) in enumerate(TERMS)}


def at_least(engine, semaphore, value):
    if isinstance(value, int) and value <= 0:
        return
    engine.wait_ge(semaphore, value)


def pipelined(engine, steps, step):
    step(0, None, 0)
    step(1, 0, 1)
    step(2, 1, 0)
    with engine.Fori(1, steps // 2 - 1) as i:
        step(i * 2 + 1, i * 2, 1)
        step(i * 2 + 2, i * 2 + 1, 0)
    step(steps - 1, steps - 2, 1)
    step(None, steps - 1, 0)


def pipelined_three(engine, steps, step):
    step(0, None, None, 1)
    step(1, 0, None, 0)
    step(2, 1, 0, 1)
    step(3, 2, 1, 0)
    with engine.Fori(1, steps // 2 - 1) as i:
        step(i * 2 + 2, i * 2 + 1, i * 2, 1)
        step(i * 2 + 3, i * 2 + 2, i * 2 + 1, 0)
    step(None, steps - 1, steps - 2, 1)
    step(None, None, steps - 1, 0)


def window_pair(image_rows, pair):
    return image_rows[:, :, 2 * GS * pair:2 * GS * (pair + 1)].rearrange("c h (w v) -> c w h v", w=2)


def score_window(slot, half):
    group, odd = divmod(slot, 2)
    return 4 * group + ((3, 1) if odd else (0, 2))[half]


def windows(in_window_order):
    return in_window_order.rearrange("c w (h v) -> c w h v", v=GS)


def mix_tokens(nc, x, x2, Wq, bq, Wk, bk, Wv, bv, W1, b1, W2, b2):
    images = x.shape[0]
    tiles = images * TILES_PER_IMAGE
    scale = 1.0 / float(C) ** 0.5
    with ExitStack() as ctx:
        def sb(name, shape, dt=FP32):
            return ctx.enter_context(nc.sbuf_tensor(name, shape, dt))

        def bank(name, banks=1):
            return ctx.enter_context(nc.psum_tensor(name, [C, banks * BANK], FP32))

        def sem(name):
            return ctx.enter_context(nc.semaphore(name))

        raw = sb("raw", [C, 7, C])
        wT = sb("wT", [C, 7, C])
        ident = sb("ident", [C, C])
        bias_q, bias_k, bias_v, bias_2 = (sb(f"bias_{n}", [C, 1]) for n in "qkv2")
        bias_1 = sb("bias_1", [C, 2])
        zero_rows = sb("zero_rows", [C, images, PAD * W])
        xt = [sb(f"xt{p}", [C, GS, W]) for p in range(2)]
        xw = sb("xw", [C, 2 * PAIRS, WIN])
        q_sb = sb("q_sb", [C, 2 * PAIRS, WIN])
        k_sb = sb("k_sb", [C, 2 * PAIRS, WIN])
        vT = [sb(f"vT{p}", [C, PAIRS, C]) for p in range(2)]
        row_max = sb("row_max", [C, PAIRS])
        row_sum = sb("row_sum", [C, PAIRS])
        row_inv = sb("row_inv", [C, PAIRS])
        scores = sb("scores", [C, PAIRS, WIN])
        expd = sb("expd", [C, PAIRS, WIN])
        probs = sb("probs", [C, PAIRS, WIN])
        probsT = sb("probsT", [C, PAIRS, C])
        x1 = sb("x1", [C, GS, W])
        hidden = sb("hidden", [C, 2, 2, BANK])
        xo = [sb(f"xo{p}", [C, GS, W]) for p in range(2)]

        ring = [bank(f"ring{p}") for p in range(2)]
        ps_s = bank("ps_s")
        ps_ta = bank("ps_ta", 2)
        ps_w2 = bank("ps_w2", 2)

        loaded = sem("loaded")
        ident_zero, ident_ready = sem("ident_zero"), sem("ident_ready")
        zeros_ready, zeros_stored = sem("zeros_ready"), sem("zeros_stored")
        wt_done, wt_ready = sem("wt_done"), sem("wt_ready")
        xw_ready = sem("xw_ready")
        x_in = [sem(f"x_in{p}") for p in range(2)]
        stored = [sem(f"stored{p}") for p in range(2)]
        qkv_done, qkv_ready = sem("qkv_done"), sem("qkv_ready")
        s_done, maxed, centred, exp_done = sem("s_done"), sem("maxed"), sem("centred"), sem("exp_done")
        summed, inverted, probs_ready = sem("summed"), sem("inverted"), sem("probs_ready")
        t_done, probsT_ready, av_done, x1_ready = sem("t_done"), sem("probsT_ready"), sem("av_done"), sem("x1_ready")
        w1_done, gelu_ready, w2_done, xo_ready = sem("w1_done"), sem("gelu_ready"), sem("w2_done"), sem("xo_ready")

        def input_count(m, p):
            return (m - p) // 2 * 16 + 16 if isinstance(m, int) else (m - p) * 8 + 16

        def half(t, h):
            return t[:, :, HALF * h:HALF * (h + 1)]

        def x_tile(n):
            first = (n % TILES_PER_IMAGE) * GS
            return x[bass.ds(n // TILES_PER_IMAGE, 1), :, bass.ds(first, GS), :].rearrange("b c h w -> (b c) h w")

        def x2_tile(n):
            first = (n % TILES_PER_IMAGE) * GS + PAD
            return x2[bass.ds(n // TILES_PER_IMAGE, 1), :, bass.ds(first, GS), :].rearrange("b c h w -> (b c) h w")

        with nc.Block() as block:
            @block.sync
            def _(sp):
                for i, w in enumerate((Wq, Wk, Wv, W1[0:C, :], W1[C:HID, :], W2[:, 0:C], W2[:, C:HID])):
                    sp.dma_start(raw[:, i, :], w).then_inc(loaded, 16)
                for t, b in ((bias_q, bq), (bias_k, bk), (bias_v, bv), (bias_2, b2)):
                    sp.dma_start(t[:, :], b.rearrange("(c a) -> c a", a=1)).then_inc(loaded, 16)
                for m in range(2):
                    sp.dma_start(bias_1[:, m:m + 1], b1[m * C:(m + 1) * C].rearrange("(c a) -> c a", a=1)).then_inc(loaded, 16)
                sp.dma_start(xt[0][:, :, :], x_tile(0)).then_inc(x_in[0], 16)
                sp.dma_start(xt[1][:, :, :], x_tile(1)).then_inc(x_in[1], 16)
                sp.wait_ge(zeros_ready, 1)
                for r in (0, H + PAD):
                    sp.dma_start(x2[:, :, r:r + PAD, :].rearrange("b c h w -> c b (h w)"), zero_rows[:, :, :]).then_inc(zeros_stored, 16)

                def load_and_store(n, p, uses, more=True):
                    if more:
                        sp.wait_ge(x1_ready, 2 * n + 2)
                        sp.dma_start(xt[p][:, :, :], x_tile(n + 2)).then_inc(x_in[p], 16)
                    sp.wait_ge(xo_ready, 2 * n + 2)
                    sp.dma_start(x2_tile(n), xo[p][:, :, :]).then_inc(stored[p], 16)

                with sp.Fori(0, tiles // 2 - 1) as i:
                    load_and_store(i * 2, 0, i)
                    load_and_store(i * 2 + 1, 1, i)
                load_and_store(tiles - 2, 0, None, more=False)
                load_and_store(tiles - 1, 1, None, more=False)
                for p in range(2):
                    sp.wait_ge(stored[p], 16 * (tiles // 2))
                sp.wait_ge(zeros_stored, 32)

            @block.gpsimd
            def _(pool):
                nc.gpsimd.memset(ident[:, :], 0.0).then_inc(ident_zero, 1)
                pool.wait_ge(ident_zero, 1)
                nc.gpsimd.affine_select(out=ident[:, :], in_=ident[:, :], compare_op=ALU.not_equal, fill=1.0, base=0,
                                        pattern=[[-1, C]], channel_multiplier=1).then_inc(ident_ready, 1)
                nc.gpsimd.memset(zero_rows[:, :, :], 0.0).then_inc(zeros_ready, 1)
                nc.gpsimd.memset(probsT[:, :, :], 0.0).then_inc(zeros_ready, 1)

            @block.tensor
            def _(pe):
                pe.wait_ge(loaded, 16 * 13)
                pe.wait_ge(ident_ready, 1)
                for i in range(7):
                    if i >= 2:
                        pe.wait_ge(wt_ready, i - 1)
                    nc.tensor.matmul(ring[i % 2][:, 0:C], raw[:, i, :], ident[:, :], is_transpose=True,
                                     start=True, stop=True).then_inc(wt_done, 1)
                pe.wait_ge(wt_ready, 7)

                def project(m, p, which):
                    if which == 0:
                        at_least(pe, x_in[p], input_count(m, p))
                    for h in range(2):
                        if which == 0 and isinstance(m, int) and m == 1:
                            pe.wait_ge(qkv_ready, 5 + h)
                        elif which == 0:
                            at_least(pe, gelu_ready, 4 * m - 5 + h)
                        else:
                            pe.wait_ge(qkv_ready, 6 * m + 1 + h)
                        nc.tensor.matmul(ring[h][:, :], wT[:, which, :], half(xt[p], h), start=True, stop=True).then_inc(qkv_done, 1)

                def values(m, p):
                    pe.wait_ge(xw_ready, m + 1)
                    for h in range(2):
                        pe.wait_ge(qkv_ready, 6 * m + 3 + h)
                        for j in range(PAIRS // 2):
                            mm = nc.tensor.matmul(ring[h][:, C * j:C * (j + 1)], xw[:, PAIRS * h + 2 * j:PAIRS * h + 2 * j + 2, :], wT[:, 2, :],
                                                  start=(j == 0), stop=(j == PAIRS // 2 - 1), skip_group_check=True)
                        mm.then_inc(qkv_done, 1)

                def window_scores(m):
                    pe.wait_ge(qkv_ready, 6 * m + 4)
                    at_least(pe, centred, m)
                    for a in range(2):
                        for j in range(PAIRS):
                            w = score_window(j, a)
                            mm = nc.tensor.matmul(ps_s[WIN * a:WIN * (a + 1), WIN * j:WIN * (j + 1)],
                                                  q_sb[:, w, :], k_sb[:, w, :],
                                                  start=(j == 0), stop=(j == PAIRS - 1), skip_group_check=True)
                    mm.then_inc(s_done, 1)

                def transpose_probs(n):
                    pe.wait_ge(probs_ready, n + 1)
                    at_least(pe, x1_ready, 2 * n - 1)
                    for g in range(PAIRS // 2):
                        mm = nc.tensor.matmul(ps_ta[:, C * g:C * (g + 1)], probs[:, 2 * g:2 * g + 2, :], ident[:, :],
                                              is_transpose=True, start=True, stop=True)
                    mm.then_inc(t_done, 1)

                def attend(n, p):
                    pe.wait_ge(probsT_ready, n + 1)
                    pe.wait_ge(qkv_ready, 6 * n + 6)
                    for h in range(2):
                        out = ps_ta[:, BANK * h:BANK * (h + 1)].rearrange("c (h w) -> c h w", h=GS)
                        for j in range(PAIRS // 2):
                            pair = h * PAIRS // 2 + j
                            mm = nc.tensor.matmul(window_pair(out, j), vT[p][:, pair, :], probsT[:, pair, :],
                                                  start=(j == 0), stop=(j == PAIRS // 2 - 1), skip_group_check=True)
                        mm.then_inc(av_done, 1)

                def mlp_up(n, front):
                    pe.wait_ge(x1_ready, 2 * n + 2)
                    for h in range(2):
                        for m in range(2):
                            if h == 1:
                                pe.wait_ge(gelu_ready, 4 * n + 1 + m)
                            elif front:
                                pe.wait_ge(qkv_ready, 6 * n + 11 + m)
                            else:
                                pe.wait_ge(gelu_ready, 4 * n - 1 + m)
                            nc.tensor.matmul(ring[m][:, :], wT[:, 3 + m, :], x1[:, 4 * h:4 * h + 4, :],
                                             start=True, stop=True).then_inc(w1_done, 1)

                def mlp_down(n):
                    for h in range(2):
                        pe.wait_ge(gelu_ready, 4 * n + 2 + 2 * h)
                        at_least(pe, xo_ready, 2 * n - 1 + h)
                        for m in range(2):
                            mm = nc.tensor.matmul(ps_w2[:, BANK * h:BANK * (h + 1)], wT[:, 5 + m, :], hidden[:, h, m, :],
                                                  start=(m == 0), stop=(m == 1))
                        mm.then_inc(w2_done, 1)

                def step(m, n, p):
                    if m is not None:
                        project(m, p, 0)
                        project(m, p, 1)
                    if n is not None:
                        transpose_probs(n)
                    if m is not None:
                        values(m, p)
                    if n is not None:
                        attend(n, 1 - p)
                    if m is not None:
                        window_scores(m)
                    if n is not None:
                        mlp_up(n, m is not None)
                        mlp_down(n)

                pipelined(pe, tiles, step)

            @block.scalar
            def _(act):
                act.wait_ge(loaded, 16 * 13)
                act.wait_ge(zeros_ready, 2)

                def step(m, n, p):
                    if m is not None:
                        at_least(act, s_done, m)
                        for i, (dst, bias) in enumerate(((q_sb, bias_q), (k_sb, bias_k))):
                            for h in range(2):
                                act.wait_ge(qkv_done, 6 * m + 2 * i + h + 1)
                                nc.scalar.activation(windows(dst[:, PAIRS * h:PAIRS * (h + 1), :]),
                                                     ring[h][:, :].rearrange("c (h w v) -> c w h v", h=GS, v=GS),
                                                     ACT.Identity, bias=bias[:, 0:1]).then_inc(qkv_ready, 1)
                    if n is not None:
                        act.wait_ge(t_done, n + 1)
                        at_least(act, av_done, 2 * n)
                        low = ps_ta[WIN:C, 0:BANK].rearrange("l (g b k) -> l g b k", b=2, k=WIN)
                        nc.scalar.activation(probsT[0:WIN, :, 0:WIN], ps_ta[0:WIN, 0:BANK].rearrange("l (j k) -> l j k", k=WIN), ACT.Copy)
                        for b in range(2):
                            a = nc.scalar.activation(probsT[WIN:C, b:PAIRS:2, WIN:C], low[:, :, 1 - b, :], ACT.Copy)
                        a.then_inc(probsT_ready, 1)
                    if m is not None:
                        for h in range(2):
                            act.wait_ge(qkv_done, 6 * m + 5 + h)
                            nc.scalar.activation(vT[p][:, 4 * h:4 * h + 4, :], ring[h][:, :].rearrange("c (h w) -> c h w", h=4),
                                                 ACT.Copy).then_inc(qkv_ready, 1)
                    if n is not None:
                        at_least(act, w2_done, 2 * n)
                        for h in range(2):
                            for i in range(2):
                                act.wait_ge(w1_done, 4 * n + 2 * h + i + 1)
                                nc.scalar.activation(hidden[:, h, i, :], ring[i][:, :], ACT.Gelu,
                                                     bias=bias_1[:, i:i + 1]).then_inc(gelu_ready, 1)
                    if m is not None:
                        act.wait_ge(centred, m + 1)
                        at_least(act, probs_ready, m)
                        nc.scalar.activation(expd[:, :, :], scores[:, :, :], ACT.Exp, scale=scale).then_inc(exp_done, 1)

                pipelined(act, tiles, step)

            @block.vector
            def _(dve):
                for i in range(7):
                    dve.wait_ge(wt_done, i + 1)
                    nc.vector.tensor_copy(wT[:, i, :], ring[i % 2][:, 0:C]).then_inc(wt_ready, 1)

                def stores_done(n, p):
                    if isinstance(n, int):
                        at_least(dve, stored[p], (n - p) // 2 * 16)
                    else:
                        dve.wait_ge(stored[p], (n - p) * 8)

                def step(m, n, p):
                    if m is not None:
                        dve.wait_ge(x_in[p], input_count(m, p))
                        at_least(dve, qkv_done, 6 * m)
                        nc.vector.tensor_copy(windows(xw[:, :, :]), xt[p][:, :, :].rearrange("c h (w v) -> c w h v", v=GS)).then_inc(xw_ready, 1)
                    if n is not None:
                        at_least(dve, w1_done, 4 * n)
                        at_least(dve, xo_ready, 2 * n)
                        for h in range(2):
                            dve.wait_ge(av_done, 2 * n + h + 1)
                            nc.vector.scalar_tensor_tensor(
                                out=half(x1, h), in0=ps_ta[:, BANK * h:BANK * (h + 1)].rearrange("c (h w) -> c h w", h=GS),
                                scalar=bias_v[:, 0:1], in1=half(xt[1 - p], h), op0=ALU.add, op1=ALU.add).then_inc(x1_ready, 1)
                    if m is not None:
                        s = ps_s[:, :].rearrange("k (j l) -> k j l", l=WIN)
                        dve.wait_ge(s_done, m + 1)
                        nc.vector.reduce_max(row_max[:, :], s, AXIS_X).then_inc(maxed, 1)
                        dve.wait_ge(maxed, m + 1)
                        at_least(dve, exp_done, m)
                        nc.vector.tensor_tensor(scores[:, :, :], s, row_max[:, :].unsqueeze(2).to_broadcast([C, PAIRS, WIN]),
                                                ALU.subtract).then_inc(centred, 1)
                    if n is not None:
                        stores_done(n, 1 - p)
                        for h in range(2):
                            dve.wait_ge(w2_done, 2 * n + h + 1)
                            nc.vector.scalar_tensor_tensor(
                                out=xo[1 - p][:, 4 * h:4 * h + 4, :], in0=ps_w2[:, BANK * h:BANK * (h + 1)].rearrange("c (h w) -> c h w", w=W),
                                scalar=bias_2[:, 0:1], in1=x1[:, 4 * h:4 * h + 4, :], op0=ALU.add, op1=ALU.add).then_inc(xo_ready, 1)
                    if m is not None:
                        dve.wait_ge(exp_done, m + 1)
                        nc.vector.reduce_sum(row_sum[:, :], expd[:, :, :], AXIS_X).then_inc(summed, 1)
                        dve.wait_ge(summed, m + 1)
                        nc.vector.reciprocal(row_inv[:, :], row_sum[:, :]).then_inc(inverted, 1)
                        dve.wait_ge(inverted, m + 1)
                        at_least(dve, t_done, m)
                        nc.vector.tensor_tensor(probs[:, :, :], expd[:, :, :], row_inv[:, :].unsqueeze(2).to_broadcast([C, PAIRS, WIN]),
                                                ALU.mult).then_inc(probs_ready, 1)

                pipelined(dve, tiles, step)


def convolve(nc, x2, out, w_pw, b_pw, w_dw, b_dw, w_g, b_g, w_att, b_att, w_211, b_211, gamma, ga1, selfb, selfw):
    images = out.shape[0]
    bands = images * BANDS_PER_IMAGE
    SLOTS = 2 * TAPS + 1
    with ExitStack() as ctx:
        ctx.enter_context(nc.allow_non_contiguous_dma(reason="small transposed weights"))

        def sb(name, shape, dt=FP32):
            return ctx.enter_context(nc.sbuf_tensor(name, shape, dt))

        def bank(name, banks=1):
            return ctx.enter_context(nc.psum_tensor(name, [C, banks * BANK], FP32))

        def sem(name):
            return ctx.enter_context(nc.semaphore(name))

        ident = sb("ident2", [C, C])
        pw_raw = sb("pw_raw", [C, C])
        pwT = sb("pwT", [C, C])
        bias_pw, bias_dw = sb("bias_pw", [C, 1]), sb("bias_dw", [C, 1])
        dw = sb("dw", [C, TAPS])
        g_raw = sb("g_raw", [C, TAPS])
        g_mask = sb("g_mask", [C, NSET])
        gT = sb("gT", [C, TAPS, 32])
        bias_h = sb("bias_h", [C, 1])
        att_raw = sb("att_raw", [C, CHUNKS, 32])
        att_gamma = sb("att_gamma", [C, CHUNKS, 32])
        attA = sb("attA", [C, CHUNKS, 32])
        attB = sb("attB", [C, CHUNKS, 32])
        gamma_col, b_att_col, bias_att = sb("gamma_col", [C, 1]), sb("b_att_col", [C, 1]), sb("bias_att", [C, 1])
        sw_raw = sb("sw_raw", [C, 2 * TAPS * C])
        sb_raw = sb("sb_raw", [C, C])
        ga_row = sb("ga_row", [C, C])
        basis_full = sb("basis_full", [C, SLOTS, C])
        basis = sb("basis", [C, SLOTS, C], FP32R)
        flag_top, flag_bottom = sb("flag_top", [C, bands]), sb("flag_bottom", [C, bands])
        bias_top, bias_bottom = sb("bias_top", [C, bands]), sb("bias_bottom", [C, bands])

        xin = [sb(f"xin{p}", [C, XROWS, WP]) for p in range(2)]
        e0 = [sb(f"e0_{p}", [C, XROWS, WP]) for p in range(2)]
        enh = [sb(f"enh{p}", [C, 2, EROWS, WP]) for p in range(2)]
        enh_x = [sb(f"enh_x{p}", [C, ROWS, W]) for p in range(2)]
        h_sb = sb("h_sb", [C, BANK])
        h_up = sb("h_up", [C, BANK])
        h_prod = sb("h_prod", [C, BANK])
        att_hi = sb("att_hi", [C, BANK], FP32R)
        att_lo = sb("att_lo", [C, BANK], FP32R)
        att = [sb(f"att{p}", [C, CHUNKS, BANK], FP32R) for p in range(2)]
        products = [sb(f"products{i}", [C, 2, BANK]) for i in range(PRODUCTS)]
        summedT = [sb(f"summedT{i}", [C, BANK]) for i in range(2)]
        out_sb = [sb(f"out_sb{p}", [C, ROWS, W]) for p in range(2)]

        ps_k = [bank(f"ps_k{i}", 2) for i in range(2)]
        ps_t = [bank(f"ps_t{i}") for i in range(2)]
        ps_f = bank("ps_f")
        ps_m = bank("ps_m")

        loaded, zeroed, ident_ready = sem("loaded2"), sem("zeroed"), sem("ident_ready2")
        mask_step, setup_step, pwT_done, basis_ready = sem("mask_step"), sem("setup_step"), sem("pwT_done"), sem("basis_ready")
        flags_ready = sem("flags_ready")
        x_in = [sem(f"band_in{p}") for p in range(2)]
        pw_done, e0_ready = sem("pw_done"), sem("e0_ready")
        conv_done, h_ready, moved, h_prod_ready = sem("conv_done"), sem("h_ready"), sem("moved"), sem("h_prod_ready")
        att_done, att_hi_ready, att_lo_ready = sem("att_done"), sem("att_hi_ready"), sem("att_lo_ready")
        att_in = [sem(f"att_in{p}") for p in range(2)]
        tap_ready, dw_done, enh_ready, enh_x_ready = sem("tap_ready"), sem("dw_done"), sem("enh_ready"), sem("enh_x_ready")
        swapped = [sem(f"swapped{p}") for p in range(2)]
        k_done, product_ready, term_done = sem("k_done"), sem("product_ready"), sem("term_done")
        sum_done, sumT_ready, back_done, out_ready = sem("sum_done"), sem("sumT_ready"), sem("back_done"), sem("out_ready")
        stored = [sem(f"band_stored{p}") for p in range(2)]

        LOADS = 7 + CHUNKS * 5 + CHUNKS + 4 * 2
        tap_sb = [t.rearrange("c (h w) -> c h w", w=W) for t in (basis_full[:, 0:2 * TAPS, :].rearrange("c s n -> c (s n)"), sw_raw[:, :])]

        def rounds(n, p, each):
            return (n - p) // 2 * each if isinstance(n, int) else (n - p) * (each // 2)

        def x_band(n):
            return x2[bass.ds(n // BANDS_PER_IMAGE, 1), :, bass.ds((n % BANDS_PER_IMAGE) * ROWS, XROWS), :].rearrange("b c h w -> (b c) h w")

        def out_band(n):
            return out[bass.ds(n // BANDS_PER_IMAGE, 1), :, bass.ds((n % BANDS_PER_IMAGE) * ROWS, ROWS), :].rearrange("b c h w -> (b c) h w")

        with nc.Block() as block:
            @block.sync
            def _(sp):
                sp.wait_ge(zeroed, 1)
                count = [0]

                def load(dst, src):
                    sp.dma_start(dst, src).then_inc(loaded, 16)
                    count[0] += 1

                def column(v):
                    return v.rearrange("(c a) -> c a", a=1)

                load(pw_raw[:, :], w_pw.rearrange("o c a b -> o (c a b)"))
                load(bias_pw[:, :], column(b_pw))
                load(bias_dw[:, :], column(b_dw))
                load(dw[:, :], w_dw.rearrange("c a h w -> c (a h w)"))
                load(g_raw[:, :], w_g.rearrange("o i h w -> (o i) (h w)"))
                load(gT[:, TAPS // 2, NSET:2 * NSET], w_211.rearrange("n c a b -> c (n a b)"))
                load(ga_row[:, :], ga1.rearrange("a c b d -> a (c b d)").to_broadcast([C, C]))
                for j in range(CHUNKS):
                    r = 32 * j
                    load(bias_h[r:r + NSET, :], column(b_g))
                    load(bias_h[r + NSET:r + 2 * NSET, :], column(b_211))
                    load(gamma_col[r:r + NSET, :], column(gamma.rearrange("a n b c -> (a n b c)")))
                    load(b_att_col[r:r + NSET, :], column(b_att))
                    load(att_raw[r:r + NSET // 2, j, 0:NSET], w_att.rearrange("n k a b -> k (n a b)"))
                for j in range(CHUNKS):
                    load(att_gamma[:, j, 0:NSET], gamma.rearrange("a n b c -> a (n b c)").to_broadcast([C, NSET]))
                for j in range(4):
                    load(sw_raw[32 * j:32 * j + NSET, :], selfw[0])
                    load(sb_raw[32 * j:32 * j + NSET, :], selfb[0])
                assert count[0] == LOADS, count[0]

                def swap_channels(m, p):
                    sp.wait_ge(enh_ready, 2 * m + 2)
                    for i in range(2):
                        sp.dma_start(enh[p][i:C:2, 1, :, :], enh[p][1 - i:C:2, 0, :, :]).then_inc(swapped[p], 16)

                def loads(m, p):
                    at_least(sp, enh_x_ready, m - 1)
                    sp.dma_start(xin[p][:, :, 1:W + 1], x_band(m)).then_inc(x_in[p], 16)

                def attention_rows(m, p):
                    sp.wait_ge(att_hi_ready, m + 1)
                    for block_row, src in ((0, att_hi), (1, att_hi), (2, att_lo), (3, att_lo)):
                        if block_row == 2:
                            sp.wait_ge(att_lo_ready, m + 1)
                        for j in range(CHUNKS):
                            sp.dma_start(att[p][32 * block_row:32 * block_row + NSET, j, :].bitcast(FP32),
                                         src[32 * j:32 * j + NSET, :].bitcast(FP32)).then_inc(att_in[p], 16)

                loads(0, 0)
                loads(1, 1)

                def full_step(m, p):
                    attention_rows(m, p)
                    swap_channels(m, p)
                    if not isinstance(m, int) or m + 2 < bands:
                        loads(m + 2, p)

                full_step(0, 0)
                full_step(1, 1)
                with sp.Fori(1, bands // 2 - 1) as i:
                    full_step(i * 2, 0)
                    full_step(i * 2 + 1, 1)
                full_step(bands - 2, 0)
                full_step(bands - 1, 1)

            @block.gpsimd
            def _(pool):
                for t in (bias_h, gamma_col, b_att_col, sb_raw):
                    nc.gpsimd.memset(t[:, :], 0.0)
                for t in (att_raw, att_gamma, attB, gT):
                    nc.gpsimd.memset(t[:, :, :], 0.0)
                nc.gpsimd.memset(sw_raw[:, :], 0.0)
                for p in range(2):
                    nc.gpsimd.memset(xin[p][:, :, :], 0.0)
                    nc.gpsimd.memset(e0[p][:, :, :], 0.0)
                    nc.gpsimd.memset(enh[p][:, :, :, :], 0.0)
                    nc.gpsimd.memset(att[p][:, :, :].bitcast(FP32), 0.0)
                for t in (flag_top, flag_bottom):
                    nc.gpsimd.memset(t[:, :], 1.0)
                nc.gpsimd.memset(g_mask[:, :], 1.0)
                nc.gpsimd.memset(ident[:, :], 0.0).then_inc(zeroed, 1)
                pool.wait_ge(zeroed, 1)
                nc.gpsimd.affine_select(out=ident[:, :], in_=ident[:, :], compare_op=ALU.not_equal, fill=1.0, base=0,
                                        pattern=[[-1, C]], channel_multiplier=1).then_inc(ident_ready, 1)
                nc.gpsimd.affine_select(out=g_mask[:, :], in_=g_mask[:, :], compare_op=ALU.is_ge, fill=0.0, base=0,
                                        pattern=[[-8, NSET]], channel_multiplier=1).then_inc(mask_step, 1)
                pool.wait_ge(mask_step, 1)
                nc.gpsimd.affine_select(out=g_mask[:, :], in_=g_mask[:, :], compare_op=ALU.is_ge, fill=0.0, base=7,
                                        pattern=[[8, NSET]], channel_multiplier=-1).then_inc(mask_step, 1)
                nc.gpsimd.affine_select(out=attB[:, :, 0:NSET], in_=attB[:, :, 0:NSET], compare_op=ALU.not_equal, fill=1.0,
                                        base=-NSET, pattern=[[-32, CHUNKS], [-1, NSET]], channel_multiplier=1).then_inc(mask_step, 1)
                nc.gpsimd.memset(flag_top[:, :].rearrange("c (b k) -> c b k", k=BANDS_PER_IMAGE)[:, :, 0:1], 0.0)
                nc.gpsimd.memset(flag_bottom[:, :].rearrange("c (b k) -> c b k", k=BANDS_PER_IMAGE)[:, :, BANDS_PER_IMAGE - 1:BANDS_PER_IMAGE],
                                 0.0).then_inc(mask_step, 1)

                def add_tap(m, p, t):
                    pool.wait_ge(tap_ready, TAPS * m + t + 1)
                    at_least(pool, dw_done, (TAPS - 1) * m + t - 1)
                    own = enh[p][:, 0, :, 1:W + 1]
                    nc.gpsimd.tensor_tensor(own, own, tap_sb[t % 2], ALU.add).then_inc(dw_done, 1)

                def store(n, p):
                    pool.wait_ge(out_ready, CHUNKS * n + CHUNKS)
                    pool.dma_start(out_band(n), out_sb[p][:, :, :]).then_inc(stored[p], 16)

                def step(l, m, n, p):
                    for t in range(1, TAPS):
                        if m is not None:
                            add_tap(m, p, t)
                        if t == 2 and n is not None and not (isinstance(n, int) and n == 0):
                            store(n - 1, p)
                    if m is not None:
                        pool.wait_ge(enh_ready, 2 * m + 2)
                        at_least(pool, sum_done, CHUNKS * (m - 1))
                        nc.gpsimd.tensor_tensor(enh_x[p][:, :, :], enh[p][:, 0, 1:ROWS + 1, 1:W + 1],
                                                xin[p][:, 2:ROWS + 2, 1:W + 1], ALU.add).then_inc(enh_x_ready, 1)

                pipelined_three(pool, bands, step)
                store(bands - 1, 1)
                for p in range(2):
                    pool.wait_ge(stored[p], 16 * (bands // 2))

            @block.tensor
            def _(pe):
                pe.wait_ge(loaded, 16 * (LOADS))
                pe.wait_ge(ident_ready, 1)
                nc.tensor.matmul(ps_m[:, 0:C], pw_raw[:, :], ident[:, :], is_transpose=True, start=True, stop=True).then_inc(pwT_done, 1)
                pe.wait_ge(basis_ready, 1)

                def pointwise(m, p, c):
                    if c == 0:
                        pe.wait_ge(x_in[p], rounds(m, p, 16) + 16)
                        at_least(pe, att_lo_ready, m)
                    else:
                        pe.wait_ge(e0_ready, PW_CHUNKS * m + c)
                    nc.tensor.matmul(ps_m[:, :], pwT[:, :], xin[p][:, CHUNK_ROWS * c:CHUNK_ROWS * (c + 1), 1:W + 1],
                                     start=True, stop=True).then_inc(pw_done, 1)

                def group_taps(m, p, first, last):
                    for i in range(first, last):
                        t, j = divmod(i, CHUNKS)
                        if i == 0:
                            pe.wait_ge(e0_ready, PW_CHUNKS * m + PW_CHUNKS)
                        dy, dx = divmod(t, 3)
                        r = 1 + CHUNK_ROWS * j + dy
                        mm = nc.tensor.matmul(ps_m[32 * j:32 * j + 32, :], gT[:, t, :], xin[p][:, r:r + CHUNK_ROWS, dx:dx + W],
                                              start=(t == 0), stop=(t == TAPS - 1))
                        if i == TAPS * CHUNKS - 1:
                            mm.then_inc(conv_done, 1)

                def coefficients(m):
                    pe.wait_ge(h_prod_ready, m + 1)
                    nc.tensor.matmul(ps_m[:, :], attA[:, :, :], h_prod[:, :], start=True, stop=False)
                    nc.tensor.matmul(ps_m[:, :], attB[:, :, :], h_sb[:, :], start=False, stop=True).then_inc(att_done, 1)

                def basis_kernels(n, p, q):
                    j, t = divmod(q, TAPS)
                    if q >= 2:
                        pe.wait_ge(product_ready, len(OPS) * n + OP_COUNT["product", q - 2])
                    else:
                        at_least(pe, product_ready, len(OPS) * (n - 1) + OP_COUNT["product", q + Q - 2])
                    for s in range(2):
                        mm = nc.tensor.matmul(ps_k[q % 2][:, BANK * s:BANK * (s + 1)], basis[:, 2 * t + s, :], att[p][:, j, :],
                                              start=True, stop=True)
                    mm.then_inc(k_done, 1)

                def add_term(n, p, kind, q):
                    j, t = divmod(q, TAPS)
                    pe.wait_ge(product_ready, len(OPS) * n + OP_COUNT[kind, q])
                    if t == 0:
                        at_least(pe, sumT_ready, CHUNKS * n + j - 1)
                    for s in range(2):
                        for r in range(CHUNK_ROWS):
                            mm = nc.tensor.matmul(ps_t[j % 2][:, C * r:C * (r + 1)], products[q % PRODUCTS][:, s, C * r:C * (r + 1)],
                                                  ident[:, :], is_transpose=True, start=(t == 0 and s == 0 and r == 0), stop=False,
                                                  skip_group_check=True)
                    mm.then_inc(term_done, 1)
                    if (kind, q) == LAST_TERM[j]:
                        if j == 0:
                            pe.wait_ge(enh_x_ready, n + 1)
                        for r in range(CHUNK_ROWS):
                            mm = nc.tensor.matmul(ps_t[j % 2][:, C * r:C * (r + 1)], enh_x[p][:, CHUNK_ROWS * j + r, :], ident[:, :],
                                                  is_transpose=True, start=False, stop=(r == CHUNK_ROWS - 1), skip_group_check=True)
                        mm.then_inc(sum_done, 1)

                def back(n, p, j):
                    at_least(pe, out_ready, CHUNKS * n + j)
                    nc.tensor.matmul(ps_f[:, :], basis[:, SLOTS - 1, :], att[p][:, j, :], start=True, stop=False, skip_group_check=True)
                    pe.wait_ge(sumT_ready, CHUNKS * n + j + 1)
                    for r in range(CHUNK_ROWS):
                        mm = nc.tensor.matmul(ps_f[:, C * r:C * (r + 1)], summedT[j % 2][:, C * r:C * (r + 1)], ident[:, :],
                                              is_transpose=True, start=False, stop=(r == CHUNK_ROWS - 1), skip_group_check=True)
                    mm.then_inc(back_done, 1)

                def first_kernels(m, p, q):
                    if q == 0:
                        pe.wait_ge(att_in[p], rounds(m, p, 256) + 256)
                    basis_kernels(m, p, q)

                def step(l, m, n, p):
                    b = 1 - p
                    for q in range(Q):
                        if n is not None and q + 2 < Q:
                            basis_kernels(n, b, q + 2)
                        elif m is not None and q + 2 >= Q:
                            first_kernels(m, p, q + 2 - Q)
                        if n is not None:
                            for kind, at in TERMS:
                                if TERM_SLOT[kind, at] == q:
                                    add_term(n, b, kind, at)
                        if m is not None:
                            if q < CONV_SLOTS:
                                group_taps(m, p, 2 * q, 2 * q + 2)
                            if q == COEFFICIENT_SLOT:
                                coefficients(m)
                        if l is not None and q in PW_SLOTS:
                            pointwise(l, b, PW_SLOTS.index(q))
                        if n is not None and q in BACK_SLOTS:
                            back(n, b, BACK_SLOTS.index(q))
                    if n is not None:
                        for kind, at in TERMS:
                            if TERM_SLOT[kind, at] == Q:
                                add_term(n, b, kind, at)
                        back(n, b, CHUNKS - 1)

                pipelined_three(pe, bands, step)

            @block.scalar
            def _(act):
                act.wait_ge(flags_ready, 1)

                def e0_rows(m, p, c):
                    act.wait_ge(pw_done, PW_CHUNKS * m + c + 1)
                    if c == 0:
                        at_least(act, tap_ready, TAPS * (m - 1))
                    ps = ps_m[:, :].rearrange("c (h w) -> c h w", w=W)
                    pieces = [(0, 4, bias_pw[:, 0:1])]
                    if c == 0:
                        pieces = [(0, 2, bias_top[:, bass.ds(m, 1)]), (2, 4, bias_pw[:, 0:1])]
                    if c == PW_CHUNKS - 1:
                        pieces = [(0, 2, bias_pw[:, 0:1]), (2, 4, bias_bottom[:, bass.ds(m, 1)])]
                    for lo, hi, bias in pieces:
                        a = nc.scalar.activation(e0[p][:, CHUNK_ROWS * c + lo:CHUNK_ROWS * c + hi, 1:W + 1], ps[:, lo:hi, :],
                                                 ACT.Identity, bias=bias)
                    a.then_inc(e0_ready, 1)

                def h_rows(m):
                    act.wait_ge(conv_done, m + 1)
                    nc.scalar.activation(h_sb[:, :], ps_m[:, :], ACT.Identity, bias=bias_h[:, 0:1]).then_inc(h_ready, 1)

                def att_high(m, p):
                    act.wait_ge(att_done, m + 1)
                    if isinstance(m, int) and m == 0:
                        pass
                    else:
                        act.wait_ge(att_in[1 - p], rounds(m - 1, 1 - p, 256) + 256)
                    nc.scalar.activation(att_hi[:, :], ps_m[:, :], ACT.Identity, bias=bias_att[:, 0:1]).then_inc(att_hi_ready, 1)

                def clear_outside(m, p):
                    act.wait_ge(dw_done, (TAPS - 1) * m + TAPS - 1)
                    for row, flag in ((0, flag_top), (EROWS - 1, flag_bottom)):
                        nc.scalar.activation(enh[p][:, 0, row, 1:W + 1], enh[p][:, 0, row, 1:W + 1], ACT.Copy,
                                             scale=flag[:, bass.ds(m, 1)]).then_inc(enh_ready, 1)

                def sum_out(n, j):
                    act.wait_ge(sum_done, CHUNKS * n + j + 1)
                    at_least(act, back_done, CHUNKS * n + j - 1)
                    nc.scalar.activation(summedT[j % 2][:, :], ps_t[j % 2][:, :], ACT.Copy).then_inc(sumT_ready, 1)

                def chunk_out(n, p, j):
                    act.wait_ge(back_done, CHUNKS * n + j + 1)
                    if j == 0:
                        at_least(act, stored[p], rounds(n, p, 16))
                    nc.scalar.activation(out_sb[p][:, CHUNK_ROWS * j:CHUNK_ROWS * (j + 1), :],
                                         ps_f[:, :].rearrange("c (h w) -> c h w", w=W), ACT.Copy).then_inc(out_ready, 1)

                def tap_product(m, p, t):
                    dy, dx = divmod(t, 3)
                    src = e0[p][:, dy:dy + EROWS, dx:dx + W]
                    if t == 0:
                        act.wait_ge(e0_ready, PW_CHUNKS * m + PW_CHUNKS)
                        at_least(act, enh_x_ready, m - 1)
                        at_least(act, swapped[p], rounds(m, p, 32))
                        at_least(act, product_ready, len(OPS) * (m - 1))
                        nc.scalar.activation(enh[p][:, 0, :, 1:W + 1], src, ACT.Identity, bias=bias_dw[:, 0:1],
                                             scale=dw[:, 0:1]).then_inc(tap_ready, 1)
                    else:
                        at_least(act, dw_done, (TAPS - 1) * m + t - 2)
                        nc.scalar.activation(tap_sb[t % 2], src, ACT.Copy, scale=dw[:, t:t + 1]).then_inc(tap_ready, 1)

                def step(l, m, n, p):
                    b = 1 - p
                    done = [0]

                    def taps(upto):
                        if m is not None:
                            for t in range(done[0], upto):
                                tap_product(m, p, t)
                        done[0] = upto

                    taps(5)
                    if n is not None:
                        sum_out(n, 0)
                    taps(6)
                    if n is not None:
                        chunk_out(n, b, 0)
                    taps(7)
                    if m is not None:
                        h_rows(m)
                    if n is not None:
                        sum_out(n, 1)
                    taps(8)
                    if m is not None:
                        att_high(m, p)
                    if n is not None:
                        chunk_out(n, b, 1)
                    taps(9)
                    if l is not None:
                        e0_rows(l, b, 0)
                        e0_rows(l, b, 1)
                    if n is not None:
                        sum_out(n, 2)
                    if l is not None:
                        e0_rows(l, b, 2)
                        e0_rows(l, b, 3)
                    if m is not None:
                        clear_outside(m, p)
                    if n is not None:
                        chunk_out(n, b, 2)
                    if l is not None:
                        e0_rows(l, b, 4)
                    if n is not None:
                        sum_out(n, 3)
                        chunk_out(n, b, 3)

                pipelined_three(act, bands, step)

            @block.vector
            def _(dve):
                dve.wait_ge(loaded, 16 * (LOADS))
                dve.wait_ge(mask_step, 4)
                for t in range(TAPS):
                    nc.vector.tensor_scalar(gT[:, t, 0:NSET], g_mask[:, :], g_raw[:, t:t + 1], None, ALU.mult)
                nc.vector.tensor_tensor(attA[:, :, :], att_raw[:, :, :], att_gamma[:, :, :], ALU.mult)
                nc.vector.tensor_tensor(bias_att[:, :], gamma_col[:, :], b_att_col[:, :], ALU.mult)
                nc.vector.tensor_scalar(bias_top[:, :], flag_top[:, :], bias_pw[:, 0:1], None, ALU.mult)
                nc.vector.tensor_scalar(bias_bottom[:, :], flag_bottom[:, :], bias_pw[:, 0:1], None, ALU.mult).then_inc(flags_ready, 1)
                ga = ga_row[:, :].rearrange("n (g i) -> n g i", i=2)
                by_group = sw_raw[:, :].rearrange("n (g m) -> n g m", m=4 * TAPS)
                for t in range(TAPS):
                    for i in range(2):
                        for s in range(2):
                            col = 2 * TAPS * i + TAPS * (i ^ s) + t
                            nc.vector.tensor_tensor(basis_full[:, 2 * t + s, :].rearrange("n (g i) -> n g i", i=2)[:, :, i:i + 1],
                                                    by_group[:, :, col:col + 1], ga[:, :, i:i + 1], ALU.mult)
                nc.vector.tensor_tensor(basis_full[:, SLOTS - 1, :], sb_raw[:, :], ga_row[:, :], ALU.mult).then_inc(setup_step, 1)
                dve.wait_ge(setup_step, 1)
                nc.vector.tensor_copy(basis[:, :, :], basis_full[:, :, :]).then_inc(setup_step, 1)
                dve.wait_ge(setup_step, 2)
                for r in (32, 96):
                    nc.vector.tensor_tensor(basis[r:r + 32, :, :], basis_full[r:r + 32, :, :], basis[r:r + 32, :, :].bitcast(FP32),
                                            ALU.subtract)
                dve.wait_ge(pwT_done, 1)
                nc.vector.tensor_copy(pwT[:, :], ps_m[:, 0:C]).then_inc(basis_ready, 1)

                def buffer_free(n, q):
                    before, at = (n, q - PRODUCTS) if q >= PRODUCTS else (n - 1, q - PRODUCTS + Q)
                    if at in TERM_OF:
                        at_least(dve, term_done, len(TERMS) * before + TERM_OF[at] + 1)
                    else:
                        at_least(dve, product_ready, len(OPS) * before + OP_COUNT["merge", at - 1])

                def product(n, p, q):
                    j, t = divmod(q, TAPS)
                    dy, dx = divmod(t, 3)
                    r = CHUNK_ROWS * j + dy
                    dve.wait_ge(k_done, Q * n + q + 1)
                    buffer_free(n, q)
                    nc.vector.tensor_tensor(products[q % PRODUCTS][:, :, :].rearrange("c s (h w) -> c s h w", w=W),
                                            ps_k[q % 2][:, :].rearrange("c (s h w) -> c s h w", s=2, w=W),
                                            enh[p][:, :, r:r + CHUNK_ROWS, dx:dx + W], ALU.mult).then_inc(product_ready, 1)

                def merge(n, q):
                    dve.wait_ge(product_ready, len(OPS) * n + OP_COUNT["product", q + 1])
                    lead = products[q % PRODUCTS]
                    nc.vector.tensor_tensor(lead[:, :, :], lead[:, :, :], products[(q + 1) % PRODUCTS][:, :, :],
                                            ALU.add).then_inc(product_ready, 1)

                def step(l, m, n, p):
                    b = 1 - p
                    if n is not None:
                        dve.wait_ge(swapped[b], rounds(n, b, 32) + 32)
                    for q in range(Q):
                        if m is not None and q == 19:
                            dve.wait_ge(h_ready, m + 1)
                        if n is not None:
                            for kind, at in OPS:
                                if kind == "product" and at == q:
                                    product(n, b, q)
                                if kind == "merge" and MERGE_SLOT[at] == q:
                                    merge(n, at)
                        if m is not None:
                            if q == 19:
                                nc.vector.stream_shuffle(h_up[:, :], h_sb[:, :],
                                                         [(i + NSET // 2) % 32 for i in range(32)]).then_inc(moved, 1)
                            if q == 20:
                                dve.wait_ge(moved, m + 1)
                                nc.vector.tensor_tensor(h_prod[:, :], h_sb[:, :], h_up[:, :], ALU.mult).then_inc(h_prod_ready, 1)
                            if q == 23:
                                dve.wait_ge(att_hi_ready, m + 1)
                                nc.vector.scalar_tensor_tensor(out=att_lo[:, :], in0=ps_m[:, :], scalar=bias_att[:, 0:1],
                                                               in1=att_hi[:, :].bitcast(FP32), op0=ALU.add,
                                                               op1=ALU.subtract).then_inc(att_lo_ready, 1)

                pipelined_three(dve, bands, step)


def build(nc, x, Wq, bq, Wk, bk, Wv, bv, W1, b1, W2, b2, w_pw, b_pw, w_dw, b_dw, w_g, b_g, w_att, b_att,
          w_211, b_211, gamma, ga1, selfb, selfw, out):
    scratch = nc.dram_tensor("layer0_out", (x.shape[0], C, H + 2 * PAD, W), FP32, kind="Internal").ap()
    mix_tokens(nc, x, scratch, Wq, bq, Wk, bk, Wv, bv, W1, b1, W2, b2)
    convolve(nc, scratch, out, w_pw, b_pw, w_dw, b_dw, w_g, b_g, w_att, b_att, w_211, b_211, gamma, ga1, selfb, selfw)


_INPUTS = ["x", "L0_conv_Wq", "L0_conv_bq", "L0_conv_Wk", "L0_conv_bk", "L0_conv_Wv", "L0_conv_bv", "L0_conv_W1",
           "L0_conv_b1", "L0_conv_W2", "L0_conv_b2", "L1_conv_w_conv1_pw", "L1_conv_b_conv1_pw", "L1_conv_w_conv1_dw",
           "L1_conv_b_conv1_dw", "L1_conv_w_conv2_g", "L1_conv_b_conv2_g", "L1_conv_w_conv2_pw", "L1_conv_b_conv2_pw",
           "L1_conv_w_conv211", "L1_conv_b_conv211", "L1_conv_attgamma", "L1_conv_ga1", "L1_conv_selfb", "L1_conv_selfw"]


def kernel(**inputs):
    import numpy as np
    import concourse.bacc as bacc
    from concourse.bass_utils import run_bass_kernel_spmd

    nc = bacc.Bacc("TRN2", target_bir_lowering=False, num_devices=1)
    arrays, args = {}, []
    for name in _INPUTS:
        a = np.ascontiguousarray(inputs[name])
        arrays[f"in_{name}"] = a
        args.append(nc.dram_tensor(f"in_{name}", a.shape, mybir.dt.from_np(a.dtype), kind="ExternalInput").ap())
    out = nc.dram_tensor("out", inputs["x"].shape, FP32, kind="ExternalOutput").ap()
    build(nc, *args, out)
    r = run_bass_kernel_spmd(nc, [arrays], core_ids=[0])
    return r.results[0]["out"]
```

```python
from contextlib import ExitStack

import concourse.bass as bass
from concourse import mybir

FP32 = mybir.dt.float32
FP32R = mybir.dt.float32r
ALU = mybir.AluOpType
ACT = mybir.ActivationFunctionType
AXIS_X = mybir.AxisListType.X

C = 128
H = W = 128
GS = 8
WIN = GS * GS
HID = 256
BANK = 512

TILES_PER_IMAGE = H // GS
PAIRS = W // GS // 2
HALF = W // 2
ROWS = 16
BANDS_PER_IMAGE = H // ROWS
PAD = 2
WP = W + 2
XROWS = ROWS + 4
EROWS = ROWS + 2
CHUNK_ROWS = BANK // W
CHUNKS = ROWS // CHUNK_ROWS
PW_CHUNKS = XROWS // CHUNK_ROWS
TAPS = 9
NSET = 16
Q = CHUNKS * TAPS
PRODUCTS = 12
TAP_BUFFERS = 4
HALVES = ((0, 10), (10, 18))

VECTOR_MERGES = (0, 3, 10, 12, 18, 21, 27, 30)
POOL_MERGES = (6, 15, 24, 33)
OPS = [op for q in range(Q) for op in [("product", q)] + [("merge", q - 2)] * (q - 2 in VECTOR_MERGES)]
OP_COUNT = {op: i + 1 for i, op in enumerate(OPS)}
PARTNERS = {q + 1 for q in VECTOR_MERGES + POOL_MERGES}
TERMS = [q for q in range(Q) if q not in PARTNERS]
VECTOR_TERMS = [q for q in TERMS if q not in POOL_MERGES]
TERM_SLOT = dict(zip(TERMS, (3, 4, 8, 9, 13, 11, 11, 16, 18, 19, 21, 19, 22, 24, 25, 26, 30, 28, 31, 33, 35, 36, 40, 37)))
FIRST_TERM = [min((TERM_SLOT[q], q) for q in TERMS if q // TAPS == j)[1] for j in range(CHUNKS)]
LAST_TERM = [max((TERM_SLOT[q], q) for q in TERMS if q // TAPS == j)[1] for j in range(CHUNKS)]
TERM_COUNT = {q: i + 1 for i, q in enumerate(sorted(VECTOR_TERMS, key=lambda q: (TERM_SLOT[q], q)))}
BACK_SLOTS = [15, 23, 32, 42]
POOL_PLACES = 2 * (TAPS - 1)
ADD_INPUT_PLACE = 1.5
ADD_SPLIT = 12
VECTOR_ADD_SLOT = 8
POOL_MERGE_PLACES = (2.6, 5.5, 10.5, 13.95)
TAP_SHIFTS = (-1.6, 0)
H_PROD_SLOT = 21
ATT_HIGH, ATT_LOW = 23.8, 25
CONV_SLOTS = [28, 28, 29, 31, 34, 34, 37, 37, 38, 39, 42, 43, 43, 46, 46, 48, 48, 50]
COEFFICIENT_SLOT = 22
PW_SLOTS = [13, 17, 20, 24, 27]


def at_least(engine, semaphore, value):
    if isinstance(value, int) and value <= 0:
        return
    engine.wait_ge(semaphore, value)


def pipelined(engine, steps, parts, step, looped=None):
    looped = looped or steps

    def peeled(s):
        step([s - k if 0 <= s - k < steps else None for k in range(parts)], s % 2)

    for s in range(4):
        peeled(s)
    with engine.Fori(2, looped // 2) as i:
        for s in range(2):
            step([i * 2 + (s - k) for k in range(parts)], s)
    for s in range(looped, steps + parts - 1):
        peeled(s)


def score_window(slot, half):
    group, odd = divmod(slot, 2)
    return 4 * group + ((3, 1) if odd else (0, 2))[half]


def windows(in_window_order):
    return in_window_order.rearrange("c w (h v) -> c w h v", v=GS)


def mix_tokens(nc, x, x2, Wq, bq, Wk, bk, Wv, bv, W1, b1, W2, b2):
    images = x.shape[0]
    tiles = images * TILES_PER_IMAGE
    scale = 1.0 / float(C) ** 0.5
    with ExitStack() as ctx:
        def sb(name, shape, dt=FP32):
            return ctx.enter_context(nc.sbuf_tensor(name, shape, dt))

        def bank(name, banks=1):
            return ctx.enter_context(nc.psum_tensor(name, [C, banks * BANK], FP32))

        def sem(name):
            return ctx.enter_context(nc.semaphore(name))

        raw = sb("raw", [C, 7, C])
        wT = sb("wT", [C, 7, C])
        w_hi, w_lo = (sb(f"w_{part}", [C, 7, C], FP32R) for part in ("hi", "lo"))
        ident = sb("ident", [C, C])
        bias_q, bias_k, bias_v, bias_2 = (sb(f"bias_{n}", [C, 1]) for n in "qkv2")
        bias_1 = sb("bias_1", [C, 2])
        zero_rows = sb("zero_rows", [C, images, PAD * W])
        xt = [sb(f"xt{p}", [C, GS, W]) for p in range(2)]
        xw = [sb(f"xw{p}", [C, 2 * PAIRS, WIN]) for p in range(2)]
        x_hi, x_lo = (sb(f"x_{part}", [C, 2 * PAIRS, WIN], FP32R) for part in ("hi", "lo"))
        q_sb = sb("q_sb", [C, 2 * PAIRS, WIN])
        k_sb = sb("k_sb", [C, 2 * PAIRS, WIN])
        vT = [sb(f"vT{p}", [C, PAIRS, C]) for p in range(2)]
        row_max = sb("row_max", [C, PAIRS])
        row_sum = sb("row_sum", [C, PAIRS])
        row_inv = sb("row_inv", [C, PAIRS])
        scores = sb("scores", [C, PAIRS, WIN])
        expd = sb("expd", [C, PAIRS, WIN])
        probs = sb("probs", [C, PAIRS, WIN])
        probsT = sb("probsT", [C, PAIRS, C])
        x1 = sb("x1", [C, 2, BANK])
        x1_hi, x1_lo = (sb(f"x1_{part}", [C, 2, BANK], FP32R) for part in ("hi", "lo"))
        x1_b2 = sb("x1_b2", [C, 2, BANK])
        hidden = sb("hidden", [C, 2, 2, BANK])
        hidden_hi, hidden_lo = (sb(f"hidden_{part}", [C, 2, 2, BANK], FP32R) for part in ("hi", "lo"))
        xo = [sb(f"xo{p}", [C, GS, W]) for p in range(2)]

        ring = [bank(f"ring{p}") for p in range(3)]
        ps_s = bank("ps_s")
        ps_ta = bank("ps_ta", 2)
        ps_w2 = bank("ps_w2", 2)

        MLP_BANKS = (2, 0, 1, 2)

        loaded = sem("loaded")
        ident_zero, ident_ready = sem("ident_zero"), sem("ident_ready")
        zeros_ready, zeros_stored = sem("zeros_ready"), sem("zeros_stored")
        wt_done, wt_ready, w_hi_ready, w_lo_ready = sem("wt_done"), sem("wt_ready"), sem("w_hi_ready"), sem("w_lo_ready")
        x_hi_ready, x_lo_ready, xw_ready = sem("x_hi_ready"), sem("x_lo_ready"), sem("xw_ready")
        x_in = [sem(f"x_in{p}") for p in range(2)]
        stored = [sem(f"stored{p}") for p in range(2)]
        qkv_done, qkv_ready = sem("qkv_done"), sem("qkv_ready")
        s_done, maxed, centred, exp_done = sem("s_done"), sem("maxed"), sem("centred"), sem("exp_done")
        summed, inverted, probs_ready = sem("summed"), sem("inverted"), sem("probs_ready")
        t_done, probsT_ready, av_done, x1_ready = sem("t_done"), sem("probsT_ready"), sem("av_done"), sem("x1_ready")
        x1_hi_ready, x1_lo_ready, x1_b2_ready = sem("x1_hi_ready"), sem("x1_lo_ready"), sem("x1_b2_ready")
        w1_done, gelu_ready, w2_done, xo_ready = sem("w1_done"), sem("gelu_ready"), sem("w2_done"), sem("xo_ready")
        hidden_hi_ready, hidden_lo_ready = sem("hidden_hi_ready"), sem("hidden_lo_ready")

        def uses(m, p, each):
            return (m - p) // 2 * each if isinstance(m, int) else (m - p) * (each // 2)

        def half_windows(in_image_order, h):
            return in_image_order[:, :, HALF * h:HALF * (h + 1)].rearrange("c h (w v) -> c w h v", v=GS)

        def x_tile(n):
            first = (n % TILES_PER_IMAGE) * GS
            return x[bass.ds(n // TILES_PER_IMAGE, 1), :, bass.ds(first, GS), :].rearrange("b c h w -> (b c) h w")

        def x2_tile(n):
            first = (n % TILES_PER_IMAGE) * GS + PAD
            return x2[bass.ds(n // TILES_PER_IMAGE, 1), :, bass.ds(first, GS), :].rearrange("b c h w -> (b c) h w")

        with nc.Block() as block:
            @block.sync
            def _(sp):
                for i, w in enumerate((Wq, Wk, Wv, W1[0:C, :], W1[C:HID, :], W2[:, 0:C], W2[:, C:HID])):
                    sp.dma_start(raw[:, i, :], w).then_inc(loaded, 16)
                for t, b in ((bias_q, bq), (bias_k, bk), (bias_v, bv), (bias_2, b2)):
                    sp.dma_start(t[:, :], b.rearrange("(c a) -> c a", a=1)).then_inc(loaded, 16)
                for m in range(2):
                    sp.dma_start(bias_1[:, m:m + 1], b1[m * C:(m + 1) * C].rearrange("(c a) -> c a", a=1)).then_inc(loaded, 16)
                sp.dma_start(xt[0][:, :, :], x_tile(0)).then_inc(x_in[0], 16)
                sp.dma_start(xt[1][:, :, :], x_tile(1)).then_inc(x_in[1], 16)
                sp.wait_ge(zeros_ready, 1)
                for r in (0, H + PAD):
                    sp.dma_start(x2[:, :, r:r + PAD, :].rearrange("b c h w -> c b (h w)"), zero_rows[:, :, :]).then_inc(zeros_stored, 16)

                def step(items, p):
                    l, m, n, d = items
                    if d is not None:
                        sp.wait_ge(xo_ready, 2 * d + 2)
                        sp.dma_start(x2_tile(d), xo[1 - p][:, :, :]).then_inc(stored[1 - p], 16)
                    if l is not None and not (isinstance(l, int) and l + 2 >= tiles):
                        sp.wait_ge(xw_ready, l + 1)
                        sp.dma_start(xt[p][:, :, :], x_tile(l + 2)).then_inc(x_in[p], 16)

                pipelined(sp, tiles, 4, step, looped=tiles - 2)
                for p in range(2):
                    sp.wait_ge(stored[p], 16 * (tiles // 2))
                sp.wait_ge(zeros_stored, 32)

            @block.gpsimd
            def _(pool):
                nc.gpsimd.memset(ident[:, :], 0.0).then_inc(ident_zero, 1)
                pool.wait_ge(ident_zero, 1)
                nc.gpsimd.affine_select(out=ident[:, :], in_=ident[:, :], compare_op=ALU.not_equal, fill=1.0, base=0,
                                        pattern=[[-1, C]], channel_multiplier=1).then_inc(ident_ready, 1)
                nc.gpsimd.memset(zero_rows[:, :, :], 0.0).then_inc(zeros_ready, 1)
                nc.gpsimd.memset(probsT[:, :, :], 0.0).then_inc(zeros_ready, 1)

                def step(items, p):
                    l, m, n, d = items
                    if d is not None:
                        for h in range(2):
                            pool.wait_ge(hidden_hi_ready, 2 * d + h + 1)
                            nc.gpsimd.tensor_tensor(hidden_lo[:, h, :, :], hidden[:, h, :, :], hidden_hi[:, h, :, :].bitcast(FP32),
                                                    ALU.subtract).then_inc(hidden_lo_ready, 1)
                    if l is not None:
                        pool.wait_ge(x_hi_ready, 2 * l + 2)
                        for h in range(2):
                            nc.gpsimd.tensor_tensor(windows(x_lo[:, PAIRS * h:PAIRS * (h + 1), :]), half_windows(xt[p], h),
                                                    windows(x_hi[:, PAIRS * h:PAIRS * (h + 1), :]).bitcast(FP32),
                                                    ALU.subtract).then_inc(x_lo_ready, 1)

                pipelined(pool, tiles, 4, step)

            @block.tensor
            def _(pe):
                pe.wait_ge(loaded, 16 * 13)
                pe.wait_ge(ident_ready, 1)
                for i in range(7):
                    if i >= 2:
                        pe.wait_ge(wt_ready, i - 1)
                    nc.tensor.matmul(ring[i % 2][:, 0:C], raw[:, i, :], ident[:, :], is_transpose=True,
                                     start=True, stop=True).then_inc(wt_done, 1)
                pe.wait_ge(wt_ready, 7)
                pe.wait_ge(w_lo_ready, 1)

                def three_passes(out, w, hi, lo, lo_ready, count, start=True, stop=True):
                    nc.tensor.matmul(out, w_hi[:, w, :], hi, start=start, stop=False)
                    nc.tensor.matmul(out, w_lo[:, w, :], hi, start=False, stop=False)
                    pe.wait_ge(lo_ready, count)
                    return nc.tensor.matmul(out, w_hi[:, w, :], lo, start=False, stop=stop)

                def project(m):
                    for i in range(4):
                        which, h = divmod(i, 2)
                        if i == 3:
                            pe.wait_ge(qkv_ready, 6 * m + 1)
                        elif isinstance(m, int) and m < 2:
                            at_least(pe, qkv_ready, m * (4 + i))
                        else:
                            pe.wait_ge(gelu_ready, 4 * m - 6 + i)
                        if which == 0:
                            pe.wait_ge(x_hi_ready, 2 * m + h + 1)
                        part = slice(PAIRS * h, PAIRS * (h + 1))
                        three_passes(ring[i % 3][:, :], which, x_hi[:, part, :], x_lo[:, part, :], x_lo_ready,
                                     2 * m + h + 1).then_inc(qkv_done, 1)

                def values(m, p, h):
                    if h == 0:
                        pe.wait_ge(xw_ready, m + 1)
                    pe.wait_ge(qkv_ready, 6 * m + 2 + h)
                    for j in range(PAIRS // 2):
                        mm = nc.tensor.matmul(ring[1 + h][:, C * j:C * (j + 1)], xw[p][:, PAIRS * h + 2 * j:PAIRS * h + 2 * j + 2, :], wT[:, 2, :],
                                              start=(j == 0), stop=(j == PAIRS // 2 - 1), skip_group_check=True)
                    mm.then_inc(qkv_done, 1)

                def window_scores(m):
                    pe.wait_ge(qkv_ready, 6 * m + 4)
                    at_least(pe, centred, m)
                    for a in range(2):
                        for j in range(PAIRS):
                            w = score_window(j, a)
                            mm = nc.tensor.matmul(ps_s[WIN * a:WIN * (a + 1), WIN * j:WIN * (j + 1)],
                                                  q_sb[:, w, :], k_sb[:, w, :],
                                                  start=(j == 0), stop=(j == PAIRS - 1), skip_group_check=True)
                    mm.then_inc(s_done, 1)

                def transpose_probs(n):
                    pe.wait_ge(probs_ready, n + 1)
                    at_least(pe, x1_ready, 2 * n)
                    for g in range(PAIRS // 2):
                        mm = nc.tensor.matmul(ps_ta[:, C * g:C * (g + 1)], probs[:, 2 * g:2 * g + 2, :], ident[:, :],
                                              is_transpose=True, start=True, stop=True)
                    mm.then_inc(t_done, 1)

                def attend(n, p):
                    pe.wait_ge(probsT_ready, n + 1)
                    pe.wait_ge(qkv_ready, 6 * n + 6)
                    for h in range(2):
                        for j in range(PAIRS // 2):
                            pair = h * PAIRS // 2 + j
                            mm = nc.tensor.matmul(ps_ta[:, C * pair:C * (pair + 1)], vT[p][:, pair, :], probsT[:, pair, :],
                                                  start=(j == 0), stop=(j == PAIRS // 2 - 1), skip_group_check=True)
                        mm.then_inc(av_done, 1)

                def mlp_up(n, front):
                    for i in range(4):
                        h, chunk = divmod(i, 2)
                        if i == 3:
                            pe.wait_ge(gelu_ready, 4 * n + 1)
                        elif front:
                            pe.wait_ge(qkv_ready, 6 * n + (12, 10, 11)[i])
                        else:
                            pe.wait_ge(gelu_ready, 4 * n - 4 + (4, 2, 3)[i])
                        if chunk == 0:
                            pe.wait_ge(x1_hi_ready, 2 * n + h + 1)
                        three_passes(ring[MLP_BANKS[i]][:, :], 3 + chunk, x1_hi[:, h, :], x1_lo[:, h, :], x1_lo_ready,
                                     2 * n + h + 1).then_inc(w1_done, 1)

                def mlp_down(n, h):
                    pe.wait_ge(hidden_hi_ready, 2 * n + h + 1)
                    at_least(pe, xo_ready, 2 * n - 1 + h)
                    for chunk in range(2):
                        mm = three_passes(ps_w2[:, BANK * h:BANK * (h + 1)], 5 + chunk, hidden_hi[:, h, chunk, :], hidden_lo[:, h, chunk, :],
                                          hidden_lo_ready, 2 * n + h + 1, start=(chunk == 0), stop=(chunk == 1))
                    mm.then_inc(w2_done, 1)

                def step(items, p):
                    l, m, n, d = items
                    if m is not None:
                        project(m)
                        values(m, 1 - p, 0)
                    if d is not None:
                        mlp_down(d, 0)
                    if m is not None:
                        values(m, 1 - p, 1)
                    if n is not None:
                        transpose_probs(n)
                    if m is not None:
                        window_scores(m)
                    if n is not None:
                        attend(n, p)
                    if d is not None:
                        mlp_down(d, 1)
                    if n is not None:
                        mlp_up(n, m is not None)

                pipelined(pe, tiles, 4, step)

            @block.scalar
            def _(act):
                act.wait_ge(loaded, 16 * 13)
                act.wait_ge(zeros_ready, 2)

                def projected(m, which, h):
                    dst, bias = ((q_sb, bias_q), (k_sb, bias_k))[which]
                    act.wait_ge(qkv_done, 6 * m + 2 * which + h + 1)
                    nc.scalar.activation(dst[:, PAIRS * h:PAIRS * (h + 1), :],
                                         ring[(2 * which + h) % 3][:, :].rearrange("c (w k) -> c w k", k=WIN),
                                         ACT.Identity, bias=bias[:, 0:1]).then_inc(qkv_ready, 1)

                def step(items, p):
                    l, m, n, d = items
                    if m is not None:
                        at_least(act, s_done, m)
                        for h in range(2):
                            projected(m, 0, h)
                    if n is not None:
                        act.wait_ge(centred, n + 1)
                        at_least(act, probs_ready, n)
                        nc.scalar.activation(expd[:, :, :], scores[:, :, :], ACT.Exp, scale=scale).then_inc(exp_done, 1)
                    if m is not None:
                        for h in range(2):
                            projected(m, 1, h)
                        for h in range(2):
                            act.wait_ge(qkv_done, 6 * m + 5 + h)
                            nc.scalar.activation(vT[1 - p][:, 4 * h:4 * h + 4, :], ring[1 + h][:, :].rearrange("c (h w) -> c h w", h=4),
                                                 ACT.Copy).then_inc(qkv_ready, 1)
                    if n is not None:
                        act.wait_ge(t_done, n + 1)
                        at_least(act, av_done, 2 * n)
                        low = ps_ta[WIN:C, 0:BANK].rearrange("l (g b k) -> l g b k", b=2, k=WIN)
                        nc.scalar.activation(probsT[0:WIN, :, 0:WIN], ps_ta[0:WIN, 0:BANK].rearrange("l (j k) -> l j k", k=WIN), ACT.Copy)
                        for b in range(2):
                            a = nc.scalar.activation(probsT[WIN:C, b:PAIRS:2, WIN:C], low[:, :, 1 - b, :], ACT.Copy)
                        a.then_inc(probsT_ready, 1)
                    if d is not None:
                        act.wait_ge(x1_ready, 2 * d + 2)
                        at_least(act, xo_ready, 2 * d)
                        nc.scalar.activation(x1_b2[:, :, :], x1[:, :, :], ACT.Identity, bias=bias_2[:, 0:1]).then_inc(x1_b2_ready, 1)
                    if n is not None:
                        for h in range(2):
                            at_least(act, hidden_lo_ready, 2 * n - 1 + h)
                            for i in range(2):
                                act.wait_ge(w1_done, 4 * n + 2 * h + i + 1)
                                nc.scalar.activation(hidden[:, h, i, :], ring[MLP_BANKS[2 * h + i]][:, :], ACT.Gelu,
                                                     bias=bias_1[:, i:i + 1]).then_inc(gelu_ready, 1)

                pipelined(act, tiles, 4, step)

            @block.vector
            def _(dve):
                for i in range(7):
                    dve.wait_ge(wt_done, i + 1)
                    nc.vector.tensor_copy(wT[:, i, :], ring[i % 2][:, 0:C]).then_inc(wt_ready, 1)
                dve.wait_ge(wt_ready, 7)
                nc.vector.tensor_copy(w_hi[:, :, :], wT[:, :, :]).then_inc(w_hi_ready, 1)
                dve.wait_ge(w_hi_ready, 1)
                nc.vector.tensor_tensor(w_lo[:, :, :], wT[:, :, :], w_hi[:, :, :].bitcast(FP32), ALU.subtract).then_inc(w_lo_ready, 1)

                def split_hidden(d):
                    for h in range(2):
                        dve.wait_ge(gelu_ready, 4 * d + 2 * h + 2)
                        at_least(dve, w2_done, 2 * d - 1 + h)
                        nc.vector.tensor_copy(hidden_hi[:, h, :, :], hidden[:, h, :, :]).then_inc(hidden_hi_ready, 1)

                def normalize(n):
                    dve.wait_ge(exp_done, n + 1)
                    nc.vector.reduce_sum(row_sum[:, :], expd[:, :, :], AXIS_X).then_inc(summed, 1)
                    dve.wait_ge(summed, n + 1)
                    nc.vector.reciprocal(row_inv[:, :], row_sum[:, :]).then_inc(inverted, 1)
                    dve.wait_ge(inverted, n + 1)
                    at_least(dve, t_done, n)
                    nc.vector.tensor_tensor(probs[:, :, :], expd[:, :, :], row_inv[:, :].unsqueeze(2).to_broadcast([C, PAIRS, WIN]),
                                            ALU.mult).then_inc(probs_ready, 1)

                def split_input(l, p):
                    dve.wait_ge(x_in[p], uses(l, p, 16) + 16)
                    at_least(dve, qkv_done, 6 * l - 2)
                    for h in range(2):
                        nc.vector.tensor_copy(windows(x_hi[:, PAIRS * h:PAIRS * (h + 1), :]), half_windows(xt[p], h)).then_inc(x_hi_ready, 1)

                def keep_input(l, p):
                    dve.wait_ge(x_lo_ready, 2 * l + 2)
                    at_least(dve, x1_ready, 2 * l - 2)
                    at_least(dve, qkv_done, 6 * l - 6)
                    nc.vector.tensor_copy(windows(xw[p][:, :, :]), xt[p][:, :, :].rearrange("c h (w v) -> c w h v", v=GS)).then_inc(xw_ready, 1)

                def add_attention(n, p):
                    at_least(dve, x1_b2_ready, n)
                    for h in range(2):
                        dve.wait_ge(av_done, 2 * n + h + 1)
                        nc.vector.scalar_tensor_tensor(
                            out=x1[:, h, :], in0=ps_ta[:, BANK * h:BANK * (h + 1)], scalar=bias_v[:, 0:1],
                            in1=xw[p][:, PAIRS * h:PAIRS * (h + 1), :].rearrange("c w k -> c (w k)"), op0=ALU.add, op1=ALU.add).then_inc(x1_ready, 1)
                        dve.wait_ge(x1_ready, 2 * n + h + 1)
                        at_least(dve, w1_done, 4 * n - 2 + 2 * h)
                        nc.vector.tensor_copy(x1_hi[:, h, :], x1[:, h, :]).then_inc(x1_hi_ready, 1)
                        dve.wait_ge(x1_hi_ready, 2 * n + h + 1)
                        nc.vector.tensor_tensor(x1_lo[:, h, :], x1[:, h, :], x1_hi[:, h, :].bitcast(FP32),
                                                ALU.subtract).then_inc(x1_lo_ready, 1)

                def add_mlp(d, p, h):
                    if h == 0:
                        dve.wait_ge(x1_b2_ready, d + 1)
                        at_least(dve, stored[p], uses(d, p, 16))
                    dve.wait_ge(w2_done, 2 * d + h + 1)
                    nc.vector.tensor_tensor(half_windows(xo[p], h), ps_w2[:, BANK * h:BANK * (h + 1)].rearrange("c (w h v) -> c w h v", h=GS, v=GS),
                                            x1_b2[:, h, :].rearrange("c (w h v) -> c w h v", h=GS, v=GS), ALU.add).then_inc(xo_ready, 1)

                def centre_scores(m):
                    s = ps_s[:, :].rearrange("k (j l) -> k j l", l=WIN)
                    dve.wait_ge(s_done, m + 1)
                    nc.vector.reduce_max(row_max[:, :], s, AXIS_X).then_inc(maxed, 1)
                    dve.wait_ge(maxed, m + 1)
                    at_least(dve, exp_done, m)
                    nc.vector.tensor_tensor(scores[:, :, :], s, row_max[:, :].unsqueeze(2).to_broadcast([C, PAIRS, WIN]),
                                            ALU.subtract).then_inc(centred, 1)

                def step(items, p):
                    l, m, n, d = items
                    if d is not None:
                        split_hidden(d)
                    if n is not None:
                        normalize(n)
                    if l is not None:
                        split_input(l, p)
                    if m is not None:
                        centre_scores(m)
                    if n is not None:
                        add_attention(n, p)
                    if d is not None:
                        add_mlp(d, 1 - p, 0)
                        add_mlp(d, 1 - p, 1)
                    if l is not None:
                        keep_input(l, p)

                pipelined(dve, tiles, 4, step)


def convolve(nc, x2, out, w_pw, b_pw, w_dw, b_dw, w_g, b_g, w_att, b_att, w_211, b_211, gamma, ga1, selfb, selfw):
    images = out.shape[0]
    bands = images * BANDS_PER_IMAGE
    SLOTS = 2 * TAPS + 1
    with ExitStack() as ctx:
        ctx.enter_context(nc.allow_non_contiguous_dma(reason="small transposed weights"))

        def sb(name, shape, dt=FP32):
            return ctx.enter_context(nc.sbuf_tensor(name, shape, dt))

        def bank(name, banks=1):
            return ctx.enter_context(nc.psum_tensor(name, [C, banks * BANK], FP32))

        def sem(name):
            return ctx.enter_context(nc.semaphore(name))

        ident = sb("ident2", [C, C])
        pw_raw = sb("pw_raw", [C, C])
        pwT = sb("pwT", [C, C])
        bias_pw, bias_dw = sb("bias_pw", [C, 1]), sb("bias_dw", [C, 1])
        dw = sb("dw", [C, TAPS])
        g_raw = sb("g_raw", [C, TAPS])
        g_mask = sb("g_mask", [C, NSET])
        gT = sb("gT", [C, TAPS, 32])
        bias_h = sb("bias_h", [C, 1])
        att_raw = sb("att_raw", [C, CHUNKS, 32])
        att_gamma = sb("att_gamma", [C, CHUNKS, 32])
        att_w = sb("att_w", [C, CHUNKS, 32])
        gamma_col, b_att_col, bias_att = sb("gamma_col", [C, 1]), sb("b_att_col", [C, 1]), sb("bias_att", [C, 1])
        sb_raw = sb("sb_raw", [C, C])
        ga_row = sb("ga_row", [C, C])
        basis = sb("basis", [C, SLOTS, C], FP32R)
        flag_top, flag_bottom = sb("flag_top", [C, bands]), sb("flag_bottom", [C, bands])
        bias_top, bias_bottom = sb("bias_top", [C, bands]), sb("bias_bottom", [C, bands])

        xin = [sb(f"xin{p}", [C, XROWS, WP]) for p in range(2)]
        e0 = [sb(f"e0_{p}", [C, XROWS, WP]) for p in range(2)]
        enh = [sb(f"enh{p}", [C, 2, EROWS, WP]) for p in range(2)]
        enh_x = sb("enh_x", [C, ROWS, W])
        tap_sb = [sb(f"tap{i}", [C, HALVES[0][1], W]) for i in range(TAP_BUFFERS)]
        h_sb = sb("h_sb", [C, BANK])
        h_up = sb("h_up", [C, BANK])
        h_prod = sb("h_prod", [C, BANK])
        att_hi = sb("att_hi", [C, BANK], FP32R)
        att_lo = sb("att_lo", [C, BANK], FP32R)
        att = [sb(f"att{p}", [C, CHUNKS, BANK], FP32R) for p in range(2)]
        products = sb("products", [C, PRODUCTS, 2, BANK])
        summedT = [sb(f"summedT{i}", [C, BANK]) for i in range(2)]
        out_sb = sb("out_sb", [C, ROWS, W])

        ps_k = [bank(f"ps_k{i}", 2) for i in range(2)]
        ps_t = [bank(f"ps_t{i}") for i in range(2)]
        ps_p = bank("ps_p")
        ps_m = bank("ps_m")

        loaded = {group: sem(f"loaded_{group}") for group in ("pointwise", "grouped", "basis")}
        zeroed, zeroed_basis, ident_ready = sem("zeroed"), sem("zeroed_basis"), sem("ident_ready2")
        pwT_ready, grouped_ready = sem("pwT_ready"), sem("grouped_ready")
        mask_step, setup_step, pwT_done, basis_ready = sem("mask_step"), sem("setup_step"), sem("pwT_done"), sem("basis_ready")
        flags_ready = sem("flags_ready")
        x_in = [sem(f"band_in{p}") for p in range(2)]
        pw_done, e0_ready = sem("pw_done"), sem("e0_ready")
        conv_done, h_ready, moved, h_prod_ready = sem("conv_done"), sem("h_ready"), sem("moved"), sem("h_prod_ready")
        att_done, att_hi_ready, att_lo_ready = sem("att_done"), sem("att_hi_ready"), sem("att_lo_ready")
        att_in = [sem(f"att_in{p}") for p in range(2)]
        tap_ready, dw_done, enh_ready, enh_x_ready = sem("tap_ready"), sem("dw_done"), sem("enh_ready"), [sem(f"enh_x_ready{i}") for i in range(2)]
        swapped = [[sem(f"swapped{p}_{h}") for h in range(2)] for p in range(2)]
        k_done, product_ready, term_done = sem("k_done"), sem("product_ready"), sem("term_done")
        pool_merged, pool_term_done = sem("pool_merged"), sem("pool_term_done")
        sum_done, sumT_ready, back_done, out_ready = sem("sum_done"), sem("sumT_ready"), sem("back_done"), sem("out_ready")
        stored = [sem(f"chunk_stored{j}") for j in range(CHUNKS)]

        LOADS, BASIS_LOADS = {"pointwise": 4, "grouped": 2 + CHUNKS * 6}, 1 + 4 * 2
        ring_memory = products[:, :, :, :].rearrange("c a s n -> c (a s n)")
        sw_raw = ring_memory[:, 0:2 * TAPS * C]
        basis_full = ring_memory[:, 2 * TAPS * C:2 * TAPS * C + SLOTS * C].rearrange("c (s n) -> c s n", n=C)

        def rounds(n, p, each):
            return (n - p) // 2 * each if isinstance(n, int) else (n - p) * (each // 2)

        def x_band(n, lo, hi):
            return x2[bass.ds(n // BANDS_PER_IMAGE, 1), :, bass.ds((n % BANDS_PER_IMAGE) * ROWS + lo, hi - lo), :].rearrange("b c h w -> (b c) h w")

        def out_chunk(n, j):
            first = (n % BANDS_PER_IMAGE) * ROWS + CHUNK_ROWS * j
            return out[bass.ds(n // BANDS_PER_IMAGE, 1), :, bass.ds(first, CHUNK_ROWS), :].rearrange("b c h w -> (b c) h w")

        with nc.Block() as block:
            @block.sync
            def _(sp):
                count = dict.fromkeys(LOADS, 0)

                def load(group, dst, src):
                    sp.dma_start(dst, src).then_inc(loaded[group], 16)
                    count[group] += 1

                def column(v):
                    return v.rearrange("(c a) -> c a", a=1)

                load("pointwise", pw_raw[:, :], w_pw.rearrange("o c a b -> o (c a b)"))
                load("pointwise", bias_pw[:, :], column(b_pw))
                load("pointwise", bias_dw[:, :], column(b_dw))
                load("pointwise", dw[:, :], w_dw.rearrange("c a h w -> c (a h w)"))
                sp.dma_start(xin[0][:, :, 1:W + 1], x_band(0, 0, XROWS)).then_inc(x_in[0], 32)
                sp.wait_ge(zeroed, 1)
                load("grouped", g_raw[:, :], w_g.rearrange("o i h w -> (o i) (h w)"))
                load("grouped", gT[:, TAPS // 2, NSET:2 * NSET], w_211.rearrange("n c a b -> c (n a b)"))
                for j in range(CHUNKS):
                    r = 32 * j
                    load("grouped", bias_h[r:r + NSET, :], column(b_g))
                    load("grouped", bias_h[r + NSET:r + 2 * NSET, :], column(b_211))
                    load("grouped", gamma_col[r:r + NSET, :], column(gamma.rearrange("a n b c -> (a n b c)")))
                    load("grouped", b_att_col[r:r + NSET, :], column(b_att))
                    load("grouped", att_raw[r:r + NSET // 2, j, 0:NSET], w_att.rearrange("n k a b -> k (n a b)"))
                    load("grouped", att_gamma[:, j, 0:NSET], gamma.rearrange("a n b c -> a (n b c)").to_broadcast([C, NSET]))
                assert count == LOADS, count

                def swap_channels(m, p, h):
                    sp.wait_ge(enh_ready, 2 * m + h + 1)
                    lo, hi = HALVES[h]
                    for i in range(2):
                        sp.dma_start(enh[p][i:C:2, 1, lo:hi, :], enh[p][1 - i:C:2, 0, lo:hi, :]).then_inc(swapped[p][h], 16)

                def loads(m, p):
                    for i, (lo, hi) in enumerate(((0, ADD_SPLIT + 2), (ADD_SPLIT + 2, XROWS))):
                        at_least(sp, enh_x_ready[i], m - 1)
                        sp.dma_start(xin[p][:, lo:hi, 1:W + 1], x_band(m, lo, hi)).then_inc(x_in[p], 16)

                def move_h2(m):
                    sp.wait_ge(h_ready, m + 1)
                    for j in range(CHUNKS):
                        sp.dma_start(h_up[32 * j:32 * j + NSET // 2, :], h_sb[32 * j + NSET // 2:32 * j + NSET, :]).then_inc(moved, 16)

                def attention_rows(m, p):
                    sp.wait_ge(att_hi_ready, m + 1)
                    for block_row, src in ((0, att_hi), (1, att_hi), (2, att_lo), (3, att_lo)):
                        if block_row == 2:
                            sp.wait_ge(att_lo_ready, m + 1)
                        for j in range(CHUNKS):
                            sp.dma_start(att[p][32 * block_row:32 * block_row + NSET, j, :].bitcast(FP32),
                                         src[32 * j:32 * j + NSET, :].bitcast(FP32)).then_inc(att_in[p], 16)

                def store(n, j):
                    sp.wait_ge(out_ready, CHUNKS * n + j + 1)
                    sp.dma_start(out_chunk(n, j), out_sb[:, CHUNK_ROWS * j:CHUNK_ROWS * (j + 1), :]).then_inc(stored[j], 16)

                def step(items, p):
                    l, m, n, o = items
                    b = 1 - p
                    if n is not None:
                        swap_channels(n, p, 1)
                    if o is not None:
                        store(o, CHUNKS - 1)
                    if l is not None and not (isinstance(l, int) and l == 0):
                        loads(l, p)
                    if m is not None:
                        move_h2(m)
                    if n is not None:
                        store(n, 0)
                    if m is not None:
                        swap_channels(m, b, 0)
                        attention_rows(m, b)
                    if n is not None:
                        store(n, 1)
                        store(n, 2)

                pipelined(sp, bands, 4, step)
                for j in range(CHUNKS):
                    sp.wait_ge(stored[j], 16 * bands)

            @block.gpsimd
            def _(pool):
                for t in (bias_h, gamma_col, b_att_col):
                    nc.gpsimd.memset(t[:, :], 0.0)
                for t in (att_raw, att_gamma, att_w, gT):
                    nc.gpsimd.memset(t[:, :, :], 0.0)
                for t in (flag_top, flag_bottom):
                    nc.gpsimd.memset(t[:, :], 1.0)
                nc.gpsimd.memset(g_mask[:, :], 1.0)
                nc.gpsimd.memset(h_up[:, :], 1.0)
                for edge in (0, WP - 1):
                    for t in xin + e0:
                        nc.gpsimd.memset(t[:, :, edge:edge + 1], 0.0)
                    for t in enh:
                        nc.gpsimd.memset(t[:, 0, :, edge:edge + 1], 0.0)
                nc.gpsimd.memset(ident[:, :], 0.0).then_inc(zeroed, 1)
                pool.wait_ge(zeroed, 1)
                nc.gpsimd.affine_select(out=ident[:, :], in_=ident[:, :], compare_op=ALU.not_equal, fill=1.0, base=0,
                                        pattern=[[-1, C]], channel_multiplier=1).then_inc(ident_ready, 1)
                nc.gpsimd.affine_select(out=g_mask[:, :], in_=g_mask[:, :], compare_op=ALU.is_ge, fill=0.0, base=0,
                                        pattern=[[-8, NSET]], channel_multiplier=1).then_inc(mask_step, 1)
                pool.wait_ge(mask_step, 1)
                nc.gpsimd.affine_select(out=g_mask[:, :], in_=g_mask[:, :], compare_op=ALU.is_ge, fill=0.0, base=7,
                                        pattern=[[8, NSET]], channel_multiplier=-1).then_inc(mask_step, 1)
                nc.gpsimd.affine_select(out=att_w[:, :, 0:NSET], in_=att_w[:, :, 0:NSET], compare_op=ALU.not_equal, fill=1.0,
                                        base=-NSET, pattern=[[-32, CHUNKS], [-1, NSET]], channel_multiplier=1).then_inc(mask_step, 1)
                nc.gpsimd.memset(flag_top[:, :].rearrange("c (b k) -> c b k", k=BANDS_PER_IMAGE)[:, :, 0:1], 0.0)
                nc.gpsimd.memset(flag_bottom[:, :].rearrange("c (b k) -> c b k", k=BANDS_PER_IMAGE)[:, :, BANDS_PER_IMAGE - 1:BANDS_PER_IMAGE],
                                 0.0).then_inc(mask_step, 1)

                def add_tap(m, p, h, t):
                    lo, hi = HALVES[h]
                    add = (TAPS - 1) * h + t - 1
                    pool.wait_ge(tap_ready, 2 * TAPS * m + TAPS * h + t + 1)
                    at_least(pool, dw_done, 2 * (TAPS - 1) * m + add)
                    own = enh[p][:, 0, lo:hi, 1:W + 1]
                    nc.gpsimd.tensor_tensor(own, own, tap_sb[add % TAP_BUFFERS][:, 0:hi - lo, :], ALU.add).then_inc(dw_done, 1)

                def add_input(n, p):
                    pool.wait_ge(dw_done, 2 * (TAPS - 1) * (n + 1))
                    at_least(pool, sum_done, CHUNKS * n)
                    nc.gpsimd.tensor_tensor(enh_x[:, 0:ADD_SPLIT, :], enh[p][:, 0, 1:ADD_SPLIT + 1, 1:W + 1],
                                            xin[p][:, 2:ADD_SPLIT + 2, 1:W + 1], ALU.add).then_inc(enh_x_ready[0], 1)

                def merge(n, index):
                    q = POOL_MERGES[index]
                    pool.wait_ge(product_ready, len(OPS) * n + OP_COUNT["product", q + 1])
                    lead = products[:, q % PRODUCTS, :, :]
                    nc.gpsimd.tensor_tensor(lead, lead, products[:, (q + 1) % PRODUCTS, :, :], ALU.add).then_inc(pool_merged, 1)

                ORDER = ([(t - 1, add_tap, 1, (0, t)) for t in range(1, TAPS)] +
                         [(TAPS - 1 + t - 1, add_tap, 1, (1, t)) for t in range(1, TAPS)] +
                         [(ADD_INPUT_PLACE, add_input, 2, ())] +
                         [(place, merge, 2, (i,)) for i, place in enumerate(POOL_MERGE_PLACES)])

                def step(items, p):
                    for place, action, part, args in sorted(ORDER, key=lambda entry: entry[0] % POOL_PLACES):
                        k = part + (place >= POOL_PLACES)
                        if items[k] is not None:
                            if action is merge:
                                action(items[k], *args)
                            else:
                                action(items[k], (p + k) % 2, *args)

                pipelined(pool, bands, 4, step)

            @block.tensor
            def _(pe):
                pe.wait_ge(loaded["pointwise"], 16 * LOADS["pointwise"])
                pe.wait_ge(ident_ready, 1)
                nc.tensor.matmul(ps_m[:, 0:C], pw_raw[:, :], ident[:, :], is_transpose=True, start=True, stop=True).then_inc(pwT_done, 1)
                pe.wait_ge(pwT_ready, 1)

                def pointwise(m, p, c):
                    if c == 0:
                        pe.wait_ge(x_in[p], rounds(m, p, 32) + 32)
                    at_least(pe, e0_ready, PW_CHUNKS * m + c)
                    nc.tensor.matmul(ps_p[:, :], pwT[:, :], xin[p][:, CHUNK_ROWS * c:CHUNK_ROWS * (c + 1), 1:W + 1],
                                     start=True, stop=True).then_inc(pw_done, 1)

                def group_taps(m, p, first, last):
                    for i in range(first, last):
                        t, j = divmod(i, CHUNKS)
                        if i == 0 and isinstance(m, int) and m == 0:
                            pe.wait_ge(grouped_ready, 1)
                        if i == 0:
                            pe.wait_ge(x_in[p], rounds(m, p, 32) + 32)
                            at_least(pe, att_lo_ready, m)
                        dy, dx = divmod(t, 3)
                        r = 1 + CHUNK_ROWS * j + dy
                        mm = nc.tensor.matmul(ps_m[32 * j:32 * j + 32, :], gT[:, t, :], xin[p][:, r:r + CHUNK_ROWS, dx:dx + W],
                                              start=(t == 0), stop=(t == TAPS - 1))
                        if i == TAPS * CHUNKS - 1:
                            mm.then_inc(conv_done, 1)

                def coefficients(m):
                    pe.wait_ge(h_prod_ready, m + 1)
                    nc.tensor.matmul(ps_m[:, :], att_w[:, :, :], h_prod[:, :], start=True, stop=True).then_inc(att_done, 1)

                def basis_kernels(n, p, q):
                    j, t = divmod(q, TAPS)
                    if q >= 2:
                        pe.wait_ge(product_ready, len(OPS) * n + OP_COUNT["product", q - 2])
                    else:
                        at_least(pe, product_ready, len(OPS) * (n - 1) + OP_COUNT["product", q + Q - 2])
                    for s in range(2):
                        mm = nc.tensor.matmul(ps_k[q % 2][:, BANK * s:BANK * (s + 1)], basis[:, 2 * t + s, :], att[p][:, j, :],
                                              start=True, stop=True)
                    mm.then_inc(k_done, 1)

                def add_term(n, q):
                    j = q // TAPS
                    if q in POOL_MERGES:
                        pe.wait_ge(pool_merged, len(POOL_MERGES) * n + POOL_MERGES.index(q) + 1)
                    else:
                        kind = "merge" if q in VECTOR_MERGES else "product"
                        pe.wait_ge(product_ready, len(OPS) * n + OP_COUNT[kind, q])
                    if q == FIRST_TERM[j]:
                        at_least(pe, out_ready, CHUNKS * n + j - 1)
                    for s in range(2):
                        for r in range(CHUNK_ROWS):
                            mm = nc.tensor.matmul(ps_t[j % 2][:, C * r:C * (r + 1)], products[:, q % PRODUCTS, s, C * r:C * (r + 1)],
                                                  ident[:, :], is_transpose=True, start=(q == FIRST_TERM[j] and s == 0 and r == 0),
                                                  stop=False, skip_group_check=True)
                    mm.then_inc(pool_term_done if q in POOL_MERGES else term_done, 1)
                    if q == LAST_TERM[j]:
                        if CHUNK_ROWS * j in (0, ADD_SPLIT):
                            pe.wait_ge(enh_x_ready[j > 0], n + 1)
                        for r in range(CHUNK_ROWS):
                            mm = nc.tensor.matmul(ps_t[j % 2][:, C * r:C * (r + 1)], enh_x[:, CHUNK_ROWS * j + r, :], ident[:, :],
                                                  is_transpose=True, start=False, stop=(r == CHUNK_ROWS - 1), skip_group_check=True)
                        mm.then_inc(sum_done, 1)

                def back(n, p, j):
                    pe.wait_ge(sumT_ready, CHUNKS * n + j + 1)
                    nc.tensor.matmul(ps_t[j % 2][:, :], basis[:, SLOTS - 1, :], att[p][:, j, :], start=True, stop=False, skip_group_check=True)
                    for r in range(CHUNK_ROWS):
                        mm = nc.tensor.matmul(ps_t[j % 2][:, C * r:C * (r + 1)], summedT[j % 2][:, C * r:C * (r + 1)], ident[:, :],
                                              is_transpose=True, start=False, stop=(r == CHUNK_ROWS - 1), skip_group_check=True)
                    mm.then_inc(back_done, 1)

                def step(items, p):
                    l, m, n, o = items
                    b = 1 - p
                    if m is None and n is None:
                        for c in range(PW_CHUNKS):
                            if l is not None:
                                pointwise(l, p, c)
                    for q in range(Q):
                        if n is not None and q + 2 < Q:
                            basis_kernels(n, p, q + 2)
                        elif m is not None and q + 2 >= Q:
                            if q + 2 == Q and isinstance(m, int) and m == 0:
                                pe.wait_ge(basis_ready, 2)
                            if q + 2 == Q:
                                pe.wait_ge(att_in[b], rounds(m, b, 256) + 256)
                            basis_kernels(m, b, q + 2 - Q)
                        for band, parity, slot in ((o, b, q + Q), (n, p, q)):
                            if band is not None:
                                for at in sorted(TERMS, key=lambda at: (TERM_SLOT[at], at)):
                                    if TERM_SLOT[at] == slot:
                                        add_term(band, at)
                                if slot in BACK_SLOTS:
                                    back(band, parity, BACK_SLOTS.index(slot))
                        for band, parity, slot in ((l, p, q), (m, b, q + Q)):
                            for k, at in enumerate(CONV_SLOTS):
                                if band is not None and at == slot:
                                    group_taps(band, parity, 2 * k, 2 * k + 2)
                        if m is not None and q == COEFFICIENT_SLOT:
                            coefficients(m)
                        if l is not None and m is not None and q in PW_SLOTS:
                            pointwise(l, p, PW_SLOTS.index(q))

                pipelined(pe, bands, 4, step)

            @block.scalar
            def _(act):
                act.wait_ge(zeroed_basis, 1)
                act.dma_start(ga_row[:, :], ga1.rearrange("a c b d -> a (c b d)").to_broadcast([C, C])).then_inc(loaded["basis"], 16)
                for j in range(4):
                    act.dma_start(sw_raw[32 * j:32 * j + NSET, :], selfw[0]).then_inc(loaded["basis"], 16)
                    act.dma_start(sb_raw[32 * j:32 * j + NSET, :], selfb[0]).then_inc(loaded["basis"], 16)
                act.wait_ge(flags_ready, 1)

                def e0_rows(m, p, c):
                    act.wait_ge(pw_done, PW_CHUNKS * m + c + 1)
                    if c == 0:
                        at_least(act, tap_ready, 2 * TAPS * (m - 1))
                    ps = ps_p[:, :].rearrange("c (h w) -> c h w", w=W)
                    pieces = [(0, 4, bias_pw[:, 0:1])]
                    if c == 0:
                        pieces = [(0, 2, bias_top[:, bass.ds(m, 1)]), (2, 4, bias_pw[:, 0:1])]
                    if c == PW_CHUNKS - 1:
                        pieces = [(0, 2, bias_pw[:, 0:1]), (2, 4, bias_bottom[:, bass.ds(m, 1)])]
                    for lo, hi, bias in pieces:
                        a = nc.scalar.activation(e0[p][:, CHUNK_ROWS * c + lo:CHUNK_ROWS * c + hi, 1:W + 1], ps[:, lo:hi, :],
                                                 ACT.Identity, bias=bias)
                    a.then_inc(e0_ready, 1)

                def h_rows(m):
                    act.wait_ge(conv_done, m + 1)
                    nc.scalar.activation(h_sb[:, :], ps_m[:, :], ACT.Identity, bias=bias_h[:, 0:1]).then_inc(h_ready, 1)

                def att_high(m, p):
                    act.wait_ge(att_done, m + 1)
                    if isinstance(m, int) and m == 0:
                        pass
                    else:
                        act.wait_ge(att_in[1 - p], rounds(m - 1, 1 - p, 256) + 256)
                    nc.scalar.activation(att_hi[:, :], ps_m[:, :], ACT.Identity, bias=bias_att[:, 0:1]).then_inc(att_hi_ready, 1)

                def clear_outside(m, p, h):
                    act.wait_ge(dw_done, (TAPS - 1) * (2 * m + h + 1))
                    row, flag = ((0, flag_top), (EROWS - 1, flag_bottom))[h]
                    nc.scalar.activation(enh[p][:, 0, row, 1:W + 1], enh[p][:, 0, row, 1:W + 1], ACT.Copy,
                                         scale=flag[:, bass.ds(m, 1)]).then_inc(enh_ready, 1)

                def sum_out(n, j):
                    act.wait_ge(sum_done, CHUNKS * n + j + 1)
                    at_least(act, back_done, CHUNKS * n + j - 1)
                    nc.scalar.activation(summedT[j % 2][:, :], ps_t[j % 2][:, :], ACT.Copy).then_inc(sumT_ready, 1)

                def chunk_out(n, j):
                    act.wait_ge(back_done, CHUNKS * n + j + 1)
                    at_least(act, stored[j], 16 * n)
                    nc.scalar.activation(out_sb[:, CHUNK_ROWS * j:CHUNK_ROWS * (j + 1), :],
                                         ps_t[j % 2][:, :].rearrange("c (h w) -> c h w", w=W), ACT.Copy).then_inc(out_ready, 1)

                def tap_product(m, p, h, t):
                    dy, dx = divmod(t, 3)
                    lo, hi = HALVES[h]
                    src = e0[p][:, lo + dy:hi + dy, dx:dx + W]
                    if t == 0:
                        if h == 0:
                            act.wait_ge(e0_ready, PW_CHUNKS * m + PW_CHUNKS)
                            at_least(act, enh_x_ready[0], m - 1)
                            for swap in swapped[p]:
                                at_least(act, swap, rounds(m, p, 32))
                            at_least(act, product_ready, len(OPS) * (m - 1))
                        nc.scalar.activation(enh[p][:, 0, lo:hi, 1:W + 1], src, ACT.Identity, bias=bias_dw[:, 0:1],
                                             scale=dw[:, 0:1]).then_inc(tap_ready, 1)
                    else:
                        add = (TAPS - 1) * h + t - 1
                        at_least(act, dw_done, 2 * (TAPS - 1) * m + add + 1 - TAP_BUFFERS)
                        nc.scalar.activation(tap_sb[add % TAP_BUFFERS][:, 0:hi - lo, :], src, ACT.Copy, scale=dw[:, t:t + 1]).then_inc(tap_ready, 1)

                TIMES = ([(at + TAP_SHIFTS[0] * (t > 3), tap_product, 1, (0, t)) for t, at in enumerate((0, 0.1, 2, 3, 10, 12, 13.5, 15, 17))] +
                         [(at + TAP_SHIFTS[1], tap_product, 1, (1, t)) for t, at in enumerate((19.5, 20, 21.5, 23, 25, 27.5, 29, 30.5, 32))] +
                         [(TERM_SLOT[LAST_TERM[j]] + 1, sum_out, 2, (j,)) for j in range(CHUNKS)] +
                         [(BACK_SLOTS[j] + 1, chunk_out, 2, (j,)) for j in range(CHUNKS)] +
                         [(at + 1, e0_rows, 0, (c,)) for c, at in enumerate(PW_SLOTS)] +
                         [(CONV_SLOTS[-1] - Q + 0.5, h_rows, 1, ()), (ATT_HIGH, att_high, 1, ()),
                          (22, clear_outside, 1, (0,)), (Q + 1, clear_outside, 1, (1,))])

                def step(items, p):
                    for at, action, part, args in sorted(TIMES, key=lambda entry: entry[0] % Q):
                        k = part + (at >= Q)
                        if items[k] is not None:
                            if action in (sum_out, chunk_out, h_rows):
                                action(items[k], *args)
                            else:
                                action(items[k], (p + k) % 2, *args)

                pipelined(act, bands, 4, step)

            @block.vector
            def _(dve):
                nc.vector.memset(sb_raw[:, :], 0.0)
                nc.vector.memset(sw_raw, 0.0).then_inc(zeroed_basis, 1)
                for p in range(2):
                    nc.vector.memset(att[p][:, :, :].bitcast(FP32), 0.0)
                dve.wait_ge(loaded["pointwise"], 16 * LOADS["pointwise"])
                dve.wait_ge(mask_step, 4)
                nc.vector.tensor_scalar(bias_top[:, :], flag_top[:, :], bias_pw[:, 0:1], None, ALU.mult)
                nc.vector.tensor_scalar(bias_bottom[:, :], flag_bottom[:, :], bias_pw[:, 0:1], None, ALU.mult).then_inc(flags_ready, 1)
                dve.wait_ge(pwT_done, 1)
                nc.vector.tensor_copy(pwT[:, :], ps_m[:, 0:C]).then_inc(pwT_ready, 1)
                dve.wait_ge(loaded["grouped"], 16 * LOADS["grouped"])
                for t in range(TAPS):
                    nc.vector.tensor_scalar(gT[:, t, 0:NSET], g_mask[:, :], g_raw[:, t:t + 1], None, ALU.mult)
                nc.vector.tensor_tensor(att_gamma[:, :, :], att_raw[:, :, :], att_gamma[:, :, :], ALU.mult).then_inc(setup_step, 1)
                dve.wait_ge(setup_step, 1)
                nc.vector.tensor_tensor(att_w[:, :, :], att_gamma[:, :, :], att_w[:, :, :], ALU.add)
                nc.vector.tensor_tensor(bias_att[:, :], gamma_col[:, :], b_att_col[:, :], ALU.mult).then_inc(grouped_ready, 1)
                dve.wait_ge(loaded["basis"], 16 * BASIS_LOADS)
                ga = ga_row[:, :].rearrange("n (g i) -> n g i", i=2)
                by_group = sw_raw[:, :].rearrange("n (g m) -> n g m", m=4 * TAPS)
                for t in range(TAPS):
                    for i in range(2):
                        for s in range(2):
                            col = 2 * TAPS * i + TAPS * (i ^ s) + t
                            nc.vector.tensor_tensor(basis_full[:, 2 * t + s, :].rearrange("n (g i) -> n g i", i=2)[:, :, i:i + 1],
                                                    by_group[:, :, col:col + 1], ga[:, :, i:i + 1], ALU.mult)
                nc.vector.tensor_tensor(basis_full[:, SLOTS - 1, :], sb_raw[:, :], ga_row[:, :], ALU.mult).then_inc(setup_step, 1)
                dve.wait_ge(setup_step, 2)
                nc.vector.tensor_copy(basis[:, :, :], basis_full[:, :, :]).then_inc(setup_step, 1)
                dve.wait_ge(setup_step, 3)
                for r in (32, 96):
                    nc.vector.tensor_tensor(basis[r:r + 32, :, :], basis_full[r:r + 32, :, :], basis[r:r + 32, :, :].bitcast(FP32),
                                            ALU.subtract).then_inc(basis_ready, 1)

                def buffer_free(n, q):
                    before, at = (n, q - PRODUCTS) if q >= PRODUCTS else (n - 1, q - PRODUCTS + Q)
                    if at in POOL_MERGES:
                        at_least(dve, pool_term_done, len(POOL_MERGES) * before + POOL_MERGES.index(at) + 1)
                    elif at in VECTOR_TERMS:
                        at_least(dve, term_done, len(VECTOR_TERMS) * before + TERM_COUNT[at])
                    elif at - 1 in POOL_MERGES:
                        at_least(dve, pool_merged, len(POOL_MERGES) * before + POOL_MERGES.index(at - 1) + 1)
                    else:
                        at_least(dve, product_ready, len(OPS) * before + OP_COUNT["merge", at - 1])

                def add_input(n, p):
                    dve.wait_ge(dw_done, 2 * (TAPS - 1) * (n + 1))
                    at_least(dve, sum_done, CHUNKS * n)
                    nc.vector.tensor_tensor(enh_x[:, ADD_SPLIT:ROWS, :], enh[p][:, 0, ADD_SPLIT + 1:ROWS + 1, 1:W + 1],
                                            xin[p][:, ADD_SPLIT + 2:ROWS + 2, 1:W + 1], ALU.add).then_inc(enh_x_ready[1], 1)

                def product(n, p, q):
                    j, t = divmod(q, TAPS)
                    dy, dx = divmod(t, 3)
                    r = CHUNK_ROWS * j + dy
                    dve.wait_ge(k_done, Q * n + q + 1)
                    buffer_free(n, q)
                    nc.vector.tensor_tensor(products[:, q % PRODUCTS, :, :].rearrange("c s (h w) -> c s h w", w=W),
                                            ps_k[q % 2][:, :].rearrange("c (s h w) -> c s h w", s=2, w=W),
                                            enh[p][:, :, r:r + CHUNK_ROWS, dx:dx + W], ALU.mult).then_inc(product_ready, 1)

                def merge(n, q):
                    dve.wait_ge(product_ready, len(OPS) * n + OP_COUNT["product", q + 1])
                    lead = products[:, q % PRODUCTS, :, :]
                    nc.vector.tensor_tensor(lead, lead, products[:, (q + 1) % PRODUCTS, :, :], ALU.add).then_inc(product_ready, 1)

                def step(items, p):
                    l, m, n, o = items
                    for q in range(Q):
                        if m is not None and q == H_PROD_SLOT:
                            dve.wait_ge(moved, 64 * (m + 1))
                        if n is not None:
                            if q in (0, 2 * TAPS):
                                dve.wait_ge(swapped[p][q > 0], rounds(n, p, 32) + 32)
                            if q == VECTOR_ADD_SLOT:
                                add_input(n, p)
                            product(n, p, q)
                            if ("merge", q - 2) in OPS:
                                merge(n, q - 2)
                        if m is not None:
                            if q == H_PROD_SLOT:
                                nc.vector.tensor_tensor(h_prod[:, :], h_sb[:, :], h_up[:, :], ALU.mult).then_inc(h_prod_ready, 1)
                            if q == ATT_LOW:
                                dve.wait_ge(att_hi_ready, m + 1)
                                nc.vector.scalar_tensor_tensor(out=att_lo[:, :], in0=ps_m[:, :], scalar=bias_att[:, 0:1],
                                                               in1=att_hi[:, :].bitcast(FP32), op0=ALU.add,
                                                               op1=ALU.subtract).then_inc(att_lo_ready, 1)

                pipelined(dve, bands, 4, step)


def build(nc, x, Wq, bq, Wk, bk, Wv, bv, W1, b1, W2, b2, w_pw, b_pw, w_dw, b_dw, w_g, b_g, w_att, b_att,
          w_211, b_211, gamma, ga1, selfb, selfw, out):
    scratch = nc.dram_tensor("layer0_out", (x.shape[0], C, H + 2 * PAD, W), FP32, kind="Internal").ap()
    mix_tokens(nc, x, scratch, Wq, bq, Wk, bk, Wv, bv, W1, b1, W2, b2)
    convolve(nc, scratch, out, w_pw, b_pw, w_dw, b_dw, w_g, b_g, w_att, b_att, w_211, b_211, gamma, ga1, selfb, selfw)


_INPUTS = ["x", "L0_conv_Wq", "L0_conv_bq", "L0_conv_Wk", "L0_conv_bk", "L0_conv_Wv", "L0_conv_bv", "L0_conv_W1",
           "L0_conv_b1", "L0_conv_W2", "L0_conv_b2", "L1_conv_w_conv1_pw", "L1_conv_b_conv1_pw", "L1_conv_w_conv1_dw",
           "L1_conv_b_conv1_dw", "L1_conv_w_conv2_g", "L1_conv_b_conv2_g", "L1_conv_w_conv2_pw", "L1_conv_b_conv2_pw",
           "L1_conv_w_conv211", "L1_conv_b_conv211", "L1_conv_attgamma", "L1_conv_ga1", "L1_conv_selfb", "L1_conv_selfw"]


def kernel(**inputs):
    import numpy as np
    import concourse.bacc as bacc
    from concourse.bass_utils import run_bass_kernel_spmd

    nc = bacc.Bacc("TRN2", target_bir_lowering=False, num_devices=1)
    arrays, args = {}, []
    for name in _INPUTS:
        a = np.ascontiguousarray(inputs[name])
        arrays[f"in_{name}"] = a
        args.append(nc.dram_tensor(f"in_{name}", a.shape, mybir.dt.from_np(a.dtype), kind="ExternalInput").ap())
    out = nc.dram_tensor("out", inputs["x"].shape, FP32, kind="ExternalOutput").ap()
    build(nc, *args, out)
    r = run_bass_kernel_spmd(nc, [arrays], core_ids=[0])
    return r.results[0]["out"]
```
